# Optimizing a Trainium2 kernel written in Bass

```python
import numpy as np
import jax
import jax.numpy as jnp

def _softmax(x, axis=-1):
    return jax.nn.softmax(x, axis=axis)

def _gelu(x):
    return jax.nn.gelu(x, approximate=True)

def _silu(x):
    return jax.nn.silu(x)

def _sigmoid(x):
    return jax.nn.sigmoid(x)

def _layernorm(x, axis=-1, eps=1e-05):
    m = jnp.mean(x, axis=axis, keepdims=True)
    v = jnp.var(x, axis=axis, keepdims=True)
    return (x - m) / jnp.sqrt(v + eps)

def _scatter_add(tgt, idx, src, axis=0):
    return tgt.at[idx].add(src)

def _segment_sum(src, seg, n):
    return jax.ops.segment_sum(src, seg, n)
kernel_name = 'mk_adj_preln_d4_adj_r2_6878c0'

def setup_inputs(seed: int=0):
    np.random.seed(seed)
    _w = jnp.asarray

    def _rec_inputs():
        import jax
        import jax.numpy as jnp
        _gk = jax.random.key(seed)
        x = 7.22e-05 + 1 * jax.random.normal(jax.random.fold_in(_gk, 1), (128, 128, 128), jnp.float32)
        _a = jax.random.bernoulli(jax.random.fold_in(_gk, 2), 0.03125, (128, 128, 128))
        _a = jnp.logical_or(_a, jnp.swapaxes(_a, -1, -2))
        _a = jnp.logical_or(_a, jnp.eye(128, dtype=bool))
        _af = _a.astype(jnp.float32)
        _af = _af * jax.random.uniform(jax.random.fold_in(_gk, 3), (128, 128, 128), jnp.float32, 0.05, 1)
        adj = _af
        _nm = jnp.ones((128, 128), dtype=bool)
        nodemask = jnp.where(_nm, 1.0, 0.0).astype(jnp.float32)
        return (x, adj, nodemask)
    x, adj, nodemask = _rec_inputs()

    def _L0_gnn_setup():
        import jax, jax.numpy as jnp
        import numpy as np
        B, N, F_IN, F_OUT = (32, 512, 128, 128)
        EPS = 1e-08
        key = jax.random.key(seed)
        k1, k2, k3 = jax.random.split(key, 3)
        x = jax.random.normal(k1, (B, N, F_IN), dtype=jnp.float32)
        adj = jax.random.uniform(k2, (B, N, N), dtype=jnp.float32)
        fan_in, fan_out = (2 * F_IN, F_OUT)
        limit = float(np.sqrt(6.0 / (fan_in + fan_out)))
        weight = jax.random.uniform(k3, (2 * F_IN, F_OUT), minval=-limit, maxval=limit, dtype=jnp.float32)
        bias = jnp.zeros((F_OUT,), dtype=jnp.float32)
        return {'x': x, 'adj': adj, 'weight': weight, 'bias': bias}
    _L0_gnn_all = _L0_gnn_setup()
    _L0_gnn_in = {k: v for k, v in _L0_gnn_all.items() if k in ('weight', 'bias')}
    del _L0_gnn_all

    def _L1_gnn_setup():
        import jax, jax.numpy as jnp
        import numpy as np
        B, N, D, C, L = (64, 256, 128, 128, 5)
        EDGE_P = 0.02

        def _gru_cell(m, h, w_ih, w_hh, b_ih, b_hh):
            gi = m @ w_ih.T + b_ih
            gh = h @ w_hh.T + b_hh
            i_r, i_z, i_n = jnp.split(gi, 3, axis=-1)
            h_r, h_z, h_n = jnp.split(gh, 3, axis=-1)
            r = jax.nn.sigmoid(i_r + h_r)
            z = jax.nn.sigmoid(i_z + h_z)
            n = jnp.tanh(i_n + r * h_n)
            return (1.0 - z) * n + z * h
        key = jax.random.key(seed)
        ks = jax.random.split(key, 8)
        x = jax.random.normal(ks[0], (B, N, D), dtype=jnp.float32)
        adj = (jax.random.uniform(ks[1], (B, N, N)) < EDGE_P).astype(jnp.float32)
        mask = jnp.ones((B, N), dtype=jnp.float32)
        s = 1.0 / np.sqrt(C).astype(np.float32)
        weight = jax.random.uniform(ks[2], (L, C, C), minval=-s, maxval=s, dtype=jnp.float32)
        w_ih = jax.random.uniform(ks[3], (3 * C, C), minval=-s, maxval=s, dtype=jnp.float32)
        w_hh = jax.random.uniform(ks[4], (3 * C, C), minval=-s, maxval=s, dtype=jnp.float32)
        b_ih = jax.random.uniform(ks[5], (3 * C,), minval=-s, maxval=s, dtype=jnp.float32)
        b_hh = jax.random.uniform(ks[6], (3 * C,), minval=-s, maxval=s, dtype=jnp.float32)
        return dict(x=x, adj=adj, mask=mask, weight=weight, w_ih=w_ih, w_hh=w_hh, b_ih=b_ih, b_hh=b_hh)
    _L1_gnn_all = _L1_gnn_setup()
    _L1_gnn_in = {k: v for k, v in _L1_gnn_all.items() if k in ('weight', 'w_ih', 'w_hh', 'b_ih', 'b_hh')}
    del _L1_gnn_all

    def _L2_gnn_setup():
        import jax, jax.numpy as jnp
        import numpy as np
        LN_EPS = 1e-05
        key = jax.random.key(seed)
        k1, k2, k3, k4 = jax.random.split(key, 4)
        B, N, F, O = (8, 1024, 128, 128)
        x = jax.random.normal(k1, (B, N, F), dtype=jnp.float32)
        adj = jax.random.uniform(k2, (B, N, N), dtype=jnp.float32)
        gamma = jnp.ones((F,), jnp.float32)
        beta = jnp.zeros((F,), jnp.float32)
        W_self = jax.random.normal(k3, (F, O), dtype=jnp.float32) * (1.0 / np.sqrt(F))
        W_neigh = jax.random.normal(k4, (F, O), dtype=jnp.float32) * (1.0 / np.sqrt(F))
        return {'x': x, 'adj': adj, 'gamma': gamma, 'beta': beta, 'W_self': W_self, 'W_neigh': W_neigh}
    _L2_gnn_all = _L2_gnn_setup()
    _L2_gnn_in = {k: v for k, v in _L2_gnn_all.items() if k in ('gamma', 'beta', 'W_self', 'W_neigh')}
    del _L2_gnn_all

    def _L3_gnn_setup():
        import jax, jax.numpy as jnp
        import numpy as np
        D_IN = 128
        D_HID = 256
        key = jax.random.key(seed)
        k1, k2, k3, k4, k5, k6 = jax.random.split(key, 6)
        x = jax.random.normal(k1, (8, 2048, D_IN), dtype=jnp.float32)
        adj = jax.random.uniform(k2, (8, 2048, 2048), dtype=jnp.float32)
        s1 = 1.0 / np.sqrt(D_IN)
        s2 = 1.0 / np.sqrt(D_HID)
        W1 = jax.random.uniform(k3, (D_IN, D_HID), dtype=jnp.float32, minval=-s1, maxval=s1)
        b1 = jax.random.uniform(k4, (D_HID,), dtype=jnp.float32, minval=-s1, maxval=s1)
        W2 = jax.random.uniform(k5, (D_HID, D_IN), dtype=jnp.float32, minval=-s2, maxval=s2)
        b2 = jax.random.uniform(k6, (D_IN,), dtype=jnp.float32, minval=-s2, maxval=s2)
        eps = jnp.zeros((1,), dtype=jnp.float32)
        return {'x': x, 'adj': adj, 'eps': eps, 'W1': W1, 'b1': b1, 'W2': W2, 'b2': b2}
    _L3_gnn_all = _L3_gnn_setup()
    _L3_gnn_in = {k: v for k, v in _L3_gnn_all.items() if k in ('eps', 'W1', 'b1', 'W2', 'b2')}
    del _L3_gnn_all
    return {'x': x, 'adj': adj, 'nodemask': nodemask, 'L0_gnn_weight': _L0_gnn_in['weight'], 'L0_gnn_bias': _L0_gnn_in['bias'], 'L1_gnn_weight': _L1_gnn_in['weight'], 'L1_gnn_w_ih': _L1_gnn_in['w_ih'], 'L1_gnn_w_hh': _L1_gnn_in['w_hh'], 'L1_gnn_b_ih': _L1_gnn_in['b_ih'], 'L1_gnn_b_hh': _L1_gnn_in['b_hh'], 'L2_gnn_gamma': _L2_gnn_in['gamma'], 'L2_gnn_beta': _L2_gnn_in['beta'], 'L2_gnn_W_self': _L2_gnn_in['W_self'], 'L2_gnn_W_neigh': _L2_gnn_in['W_neigh'], 'L3_gnn_eps': _L3_gnn_in['eps'], 'L3_gnn_W1': _L3_gnn_in['W1'], 'L3_gnn_b1': _L3_gnn_in['b1'], 'L3_gnn_W2': _L3_gnn_in['W2'], 'L3_gnn_b2': _L3_gnn_in['b2']}

def reference(x, adj, nodemask, L0_gnn_weight, L0_gnn_bias, L1_gnn_weight, L1_gnn_w_ih, L1_gnn_w_hh, L1_gnn_b_ih, L1_gnn_b_hh, L2_gnn_gamma, L2_gnn_beta, L2_gnn_W_self, L2_gnn_W_neigh, L3_gnn_eps, L3_gnn_W1, L3_gnn_b1, L3_gnn_W2, L3_gnn_b2):
    import jax
    import jax.numpy as jnp

    def _L0_gnn_ref(x, adj, weight, bias):
        import jax, jax.numpy as jnp
        import numpy as np
        B, N, F_IN, F_OUT = (32, 512, 128, 128)
        EPS = 1e-08
        adj_norm = adj / (jnp.sum(adj, axis=-1, keepdims=True) + EPS)
        h_neigh = jnp.einsum('bnm,bmf->bnf', adj_norm, x)
        h_concat = jnp.concatenate([x, h_neigh], axis=-1)
        h = jnp.einsum('bnk,ko->bno', h_concat, weight) + bias
        return jax.nn.relu(h)

    def _L1_gnn_ref(x, adj, mask, weight, w_ih, w_hh, b_ih, b_hh):
        import jax, jax.numpy as jnp
        import numpy as np
        B, N, D, C, L = (64, 256, 128, 128, 5)
        EDGE_P = 0.02

        def _gru_cell(m, h, w_ih, w_hh, b_ih, b_hh):
            gi = m @ w_ih.T + b_ih
            gh = h @ w_hh.T + b_hh
            i_r, i_z, i_n = jnp.split(gi, 3, axis=-1)
            h_r, h_z, h_n = jnp.split(gh, 3, axis=-1)
            r = jax.nn.sigmoid(i_r + h_r)
            z = jax.nn.sigmoid(i_z + h_z)
            n = jnp.tanh(i_n + r * h_n)
            return (1.0 - z) * n + z * h
        A = (adj != 0).astype(x.dtype)
        h = x
        for l in range(weight.shape[0]):
            m = jnp.einsum('bnd,de->bne', h, weight[l])
            agg = jnp.einsum('bij,bid->bjd', A, m)
            h = _gru_cell(agg, h, w_ih, w_hh, b_ih, b_hh)
        return h * mask[..., None]

    def _L2_gnn_ref(x, adj, gamma, beta, W_self, W_neigh):
        import jax, jax.numpy as jnp
        import numpy as np
        LN_EPS = 1e-05
        mu = jnp.mean(x, axis=-1, keepdims=True)
        var = jnp.mean(jnp.square(x - mu), axis=-1, keepdims=True)
        xn = (x - mu) * jax.lax.rsqrt(var + LN_EPS) * gamma + beta
        d_out = jnp.sum(adj, axis=1)
        d_in = jnp.sum(adj, axis=2)
        s_out = jnp.where(d_out != 0, jax.lax.rsqrt(d_out), 0.0)
        s_in = jnp.where(d_in != 0, jax.lax.rsqrt(d_in), 0.0)
        A_norm = s_out[:, :, None] * adj * s_in[:, None, :]
        eye = jnp.eye(adj.shape[1], dtype=adj.dtype)
        L = eye[None, :, :] - A_norm
        neighbor = jnp.einsum('bij,bjf->bif', L, xn)
        pre = xn @ W_self + neighbor @ W_neigh
        return jax.nn.softplus(pre)

    def _L3_gnn_ref(x, adj, eps, W1, b1, W2, b2):
        import jax, jax.numpy as jnp
        import numpy as np
        D_IN = 128
        D_HID = 256
        aggregated = jnp.einsum('bnm,bmd->bnd', adj, x)
        h = (1.0 + eps) * x + aggregated
        h = jax.nn.relu(h @ W1 + b1)
        return h @ W2 + b2
    h = jnp.maximum(_layernorm(x, axis=-1), 0.0)
    x = x + _L0_gnn_ref(h, adj, L0_gnn_weight, L0_gnn_bias)
    h = jnp.maximum(_layernorm(x, axis=-1), 0.0)
    x = x + _L1_gnn_ref(h, adj, nodemask, L1_gnn_weight, L1_gnn_w_ih, L1_gnn_w_hh, L1_gnn_b_ih, L1_gnn_b_hh)
    h = jnp.maximum(_layernorm(x, axis=-1), 0.0)
    x = x + _L2_gnn_ref(h, adj, L2_gnn_gamma, L2_gnn_beta, L2_gnn_W_self, L2_gnn_W_neigh)
    h = jnp.maximum(_layernorm(x, axis=-1), 0.0)
    x = x + _L3_gnn_ref(h, adj, L3_gnn_eps, L3_gnn_W1, L3_gnn_b1, L3_gnn_W2, L3_gnn_b2)
    return x

_drawn_inputs = setup_inputs


def setup_inputs(seed=0):
    import zlib

    import numpy as np

    out = dict(_drawn_inputs(seed))
    spreads = {'L0_gnn_bias': (0.0, 0.1), 'L2_gnn_gamma': (1.0, 0.2), 'L2_gnn_beta': (0.0, 0.1)}
    factors = {'L3_gnn_b1': 6.214, 'L3_gnn_b2': 2.856}
    for name, (base, spread) in spreads.items():
        noise = np.random.default_rng([zlib.crc32(name.encode()), seed]).standard_normal(out[name].shape)
        drawn = base * np.exp(spread * noise) if base else spread * noise
        out[name] = jnp.asarray(drawn.astype(out[name].dtype))
    for name, factor in factors.items():
        out[name] = (out[name] * factor).astype(out[name].dtype)
    return out
```

```python
from contextlib import ExitStack

import concourse.bass as bass
from concourse import mybir
from concourse.alu_op_type import AluOpType as ALU

F32 = mybir.dt.float32
F16 = mybir.dt.float16
I32 = mybir.dt.int32
ACT = mybir.ActivationFunctionType
AX = mybir.AxisListType.X

P = 128
GRAPHS = 128
GB = 4
NG = GRAPHS // GB
W = GB * P
LAYERS = 5
GATES = 3
LN_EPS = 1e-5
ROW_EPS = 1e-8
SH = 32.0
SW = 256.0
SLOTS = 4
ROUND = SLOTS
QUAD = LAYERS * ROUND
NQ = NG // SLOTS


def after(eng, sem, value):
    if not (isinstance(value, int) and value <= 0):
        eng.wait_ge(sem, value)


def staggered(eng, stages):
    head = max(lag for lag, _ in stages) + 2
    head += head % 2

    def plain(t):
        for lag, stage in stages:
            if 0 <= t - lag < NG:
                stage((t - lag) // 2, (t - lag) % 2)

    for t in range(head):
        plain(t)
    with eng.Fori(0, (NG - head) // 2) as i:
        for u in range(2):
            for lag, stage in stages:
                k = head + u - lag
                stage(i + k // 2, k % 2)
    for t in range(NG, NG + head):
        plain(t)


def cols(tile, g, j=None):
    return tile[:, bass.ds(g * W, W)] if j is None else tile[:, bass.ds(g * W + j * P, P)]


def graphs(ap):
    return ap.rearrange("p (b d) -> p b d", b=GB)


def prepare(nc, c):
    with ExitStack() as ctx:
        sb = lambda name, shape, dt=F32: ctx.enter_context(nc.sbuf_tensor(name, shape, dt))
        sem = lambda name: ctx.enter_context(nc.semaphore(name))
        msgT = sb("msgT", [P, LAYERS, P])
        ihT = sb("ihT", [P, GATES * P])
        wide = sb("wide", [P, LAYERS + 1, GATES * P])
        ext = sb("ext", [P, 2])
        ext_all = sb("ext_all", [P, 2])
        top = sb("top", [P, 4])
        wscale = sb("wscale", [P, 1])
        bih = sb("bih", [P, GATES])
        bhh = sb("bhh", [P, GATES])
        fold = [ctx.enter_context(nc.psum_tensor(f"fold{l}", [P, W], F32)) for l in range(LAYERS)]
        loaded, ident0, folded = sem("w_loaded"), sem("ident0"), sem("folded")
        ident_ok, copied, extremes, spread = sem("ident_ok"), sem("copied"), sem("extremes"), sem("spread")
        link, done = sem("w_link"), sem("w_done")
        block = ctx.enter_context(nc.Block())

        @block.sync
        def _(sp):
            for dst, src in ((msgT[:], c["msgT_in"].rearrange("l k c -> k l c")), (ihT[:], c["ihT_in"]),
                             (wide[:, LAYERS, :], c["hhT_in"]), (bih[:], c["bih_in"]), (bhh[:], c["bhh_in"]),
                             (c["mask"][:], c["mask_in"])):
                sp.dma_start(dst, src).then_inc(loaded, 16)

        @block.gpsimd
        def _(pool):
            nc.gpsimd.memset(c["ident"][:], 0.0).then_inc(ident0, 1)
            pool.wait_ge(ident0, 1)
            nc.gpsimd.affine_select(out=c["ident"][:], in_=c["ident"][:], compare_op=ALU.not_equal, fill=1.0,
                                    base=0, pattern=[[-1, P]], channel_multiplier=1).then_inc(ident_ok, 1)
            pool.wait_ge(extremes, 2)
            nc.gpsimd.partition_all_reduce(ext_all[:], ext[:], P,
                                           bass.bass_isa.ReduceOp.absmax).then_inc(spread, 1)

        @block.tensor
        def _(pe):
            pe.wait_ge(loaded, 6 * 16)
            for l in range(LAYERS):
                nc.tensor.matmul(fold[l][:, 0:GATES * P], msgT[:, l, :], ihT[:], start=True, stop=True)\
                  .then_inc(folded, 1)

        @block.vector
        def _(dve):
            count = [0]

            def linked(ins):
                count[0] += 1
                ins.then_inc(link, 1)
                dve.wait_ge(link, count[0])

            nc.vector.memset(c["minus_half"][:], -0.5)
            nc.vector.memset(c["ones"][:], 1.0)
            dve.wait_ge(loaded, 6 * 16)
            for l in range(LAYERS):
                dve.wait_ge(folded, l + 1)
                last = nc.vector.tensor_copy(wide[:, l, :], fold[l][:, 0:GATES * P])
            linked(last)
            flat = wide[:].rearrange("p l e -> p (l e)")
            nc.vector.tensor_reduce(ext[:, 0:1], flat, AX, ALU.max).then_inc(extremes, 1)
            nc.vector.tensor_reduce(ext[:, 1:2], flat, AX, ALU.min).then_inc(extremes, 1)
            dve.wait_ge(spread, 1)
            linked(nc.vector.tensor_tensor(top[:, 1:2], ext_all[:, 0:1], ext_all[:, 1:2], ALU.max))
            linked(nc.vector.tensor_scalar(top[:, 2:3].bitcast(I32), top[:, 1:2].bitcast(I32), 0x7F800000, None,
                                           ALU.bitwise_and))
            linked(nc.vector.tensor_scalar(top[:, 0:1], top[:, 2:3], 2.0 ** -60, None, ALU.max))
            linked(nc.vector.reciprocal(top[:, 3:4], top[:, 0:1]))
            linked(nc.vector.tensor_scalar(wscale[:], top[:, 3:4], SW, None, ALU.mult))
            nc.vector.tensor_scalar(c["gscale"][:], top[:, 0:1], 1.0 / (SW * SH), None, ALU.mult)
            nc.vector.tensor_scalar(c["bhn"][:], bhh[:, 2:3], wscale[:], SH, ALU.mult, ALU.mult)
            nc.vector.tensor_tensor(c["brz"][:], bih[:, 0:2], bhh[:, 0:2], ALU.add)
            nc.vector.tensor_copy(c["bin"][:], bih[:, 2:3])
            hi, lo = (c[n][:].rearrange("p l e -> p (l e)") for n in ("w_hi", "w_lo"))
            linked(nc.vector.tensor_scalar(hi, flat, wscale[:], None, ALU.mult))
            nc.vector.scalar_tensor_tensor(lo, flat, wscale[:], hi, ALU.mult, ALU.subtract).then_inc(done, 1)
            dve.wait_ge(done, 1)


def norm_statistics(nc, dve, x_of, stats, mv, var, stats_done, moments_done, var_ready, nth):
    for j in range(GB):
        last = nc.vector.bn_stats(stats[:, j, :], x_of(j))
    last.then_inc(stats_done, 1)
    dve.wait_ge(stats_done, nth)
    nc.vector.nop(nofuse=True)
    for j in range(GB):
        last = nc.vector.bn_aggr(mv[:, j, :], stats[:, j, :])
    last.then_inc(moments_done, 1)
    dve.wait_ge(moments_done, nth)
    nc.vector.tensor_scalar(var, mv[:, :, 1], LN_EPS, None, ALU.add).then_inc(var_ready, 1)


def layer0(nc, c):
    x, adjT, pattern, sums = c["x"], c["adjT"], c["pattern"], c["sums"]
    with ExitStack() as ctx:
        sb = lambda name, shape, dt=F32: ctx.enter_context(nc.sbuf_tensor(name, shape, dt))
        sem = lambda name: ctx.enter_context(nc.semaphore(name))
        pair = lambda name, shape, dt=F32: [sb(f"{name}{b}", shape, dt) for b in range(2)]
        ps = lambda name, shape: ctx.enter_context(nc.psum_tensor(name, shape, F32))
        wcat = sb("l0_wcat", [P, 2, P])
        bias = sb("l0_bias", [P, GB, P])
        adj = pair("l0_adj", [P, GB, P])
        hn = pair("l0_hn", [P, GB, P])
        hT = pair("l0_hT", [P, GB, P])
        aT = pair("l0_aT", [P, GB, P])
        u = pair("l0_u", [P, GB, P])
        pre = pair("l0_pre", [P, GB, P])
        stats = pair("l0_stats", [P, GB, 6])
        mv = pair("l0_mv", [P, GB, 2])
        var = pair("l0_var", [P, GB])
        rstd = pair("l0_rstd", [P, GB])
        rinv = pair("l0_rinv", [P, GB])
        psA, psH = ps("l0_psA", [P, GB, P]), ps("l0_psH", [P, GB, P])
        ps1 = [ps(f"l0_ps1{b}", [P, GB, 2 * P]) for b in range(2)]
        ps2, psS = ps("l0_ps2", [P, GB, P]), ps("l0_psS", [P, W])
        w_loaded = sem("l0_w_loaded")
        loaded = [sem(f"l0_loaded{b}") for b in range(2)]
        (stats_done, moments_done, var_ready, rstd_ready, rows_ready, pattern_done, rows_turned, adj_turned,
         hT_done, aT_done, first_done, sums_ready, u_done, sums_done, bias_done, row_done, second_done,
         gathered, x_done, kept, rinv_done) = (
            sem("l0_" + n) for n in (
                "stats_done moments_done var_ready rstd_ready rows_ready pattern_done rows_turned adj_turned "
                "hT_done aT_done first_done sums_ready u_done sums_done bias_done row_done second_done "
                "gathered x_done kept rinv_done").split())
        block = ctx.enter_context(nc.Block())

        @block.sync
        def _(sp):
            sp.dma_start(wcat[:], c["l0_w_in"].rearrange("(t k) o -> k t o", t=2)).then_inc(w_loaded, 16)
            sp.dma_start(bias[:], c["l0_b_in"].rearrange("p (b d) -> p b d", b=GB)).then_inc(w_loaded, 16)

            def load(h, b):
                g = 2 * h + b
                after(sp, sums_ready, g - 1)
                after(sp, pattern_done, g - 1)
                sp.dma_start(graphs(cols(x, g)), c["x_in"][bass.ts(g, GB)].rearrange("b n d -> n b d"))\
                  .then_inc(loaded[b], 16)
                sp.dma_start(adj[b][:], c["adj_in"][bass.ts(g, GB)].rearrange("b n d -> n b d"))\
                  .then_inc(loaded[b], 16)

            staggered(sp, [(0, load)])

        @block.gpsimd
        def _(pool):
            def root(h, b):
                pool.wait_ge(var_ready, 2 * h + b + 1)
                nc.gpsimd.tensor_tensor(rstd[b][:], var[b][:], c["minus_half"][:], ALU.pow).then_inc(rstd_ready, 1)

            def keep(h, b):
                g = 2 * h + b
                pool.wait_ge(aT_done, g + 1)
                nc.gpsimd.tensor_copy(graphs(cols(adjT, g)), aT[b][:]).then_inc(kept, 1)

            staggered(pool, [(0, root), (2, keep)])

        @block.vector
        def _(dve):
            def front(h, b):
                g = 2 * h + b
                dve.wait_ge(loaded[b], 32 * (h + 1))
                norm_statistics(nc, dve, lambda j: cols(x, g, j), stats[b], mv[b], var[b][:],
                                stats_done, moments_done, var_ready, g + 1)

            def rows(h, b):
                g = 2 * h + b
                dve.wait_ge(rstd_ready, g + 1)
                after(dve, rows_turned, g - 1)
                for j in range(GB):
                    last = nc.vector.tensor_scalar(hn[b][:, j, :], cols(x, g, j), mv[b][:, j, 0:1],
                                                   rstd[b][:, j:j + 1], ALU.subtract, ALU.mult)
                last.then_inc(rows_ready, 1)
                nc.vector.tensor_scalar(graphs(cols(pattern, g)), adj[b][:], 0.0, None, ALU.not_equal)\
                  .then_inc(pattern_done, 1)

            def middle(h, b):
                g = 2 * h + b
                dve.wait_ge(u_done, g + 1)
                nc.vector.tensor_tensor(pre[b][:], ps1[b][:, :, 0:P], bias[:], ALU.add).then_inc(bias_done, 1)
                dve.wait_ge(sums_done, g + 1)
                nc.vector.tensor_scalar(rinv[b][:], sums[:, bass.ds(g * 2 * GB, GB)], ROW_EPS, None, ALU.add)\
                  .then_inc(row_done, 1)
                dve.wait_ge(row_done, g + 1)
                nc.vector.reciprocal(rinv[b][:], rinv[b][:]).then_inc(rinv_done, 1)

            def finish(h, b):
                g = 2 * h + b
                dve.wait_ge(second_done, g + 1)
                dve.wait_ge(rinv_done, g + 1)
                for j in range(GB):
                    last = nc.vector.scalar_tensor_tensor(pre[b][:, j, :], ps2[:, j, :], rinv[b][:, j:j + 1],
                                                          pre[b][:, j, :], ALU.mult, ALU.add)
                last.then_inc(gathered, 1)
                dve.wait_ge(gathered, g + 1)
                nc.vector.scalar_tensor_tensor(cols(x, g), pre[b][:].rearrange("p b d -> p (b d)"), 0.0,
                                               cols(x, g), ALU.max, ALU.add).then_inc(x_done, 1)

            dve.wait_ge(w_loaded, 32)
            staggered(dve, [(1, rows), (4, finish), (3, middle), (0, front)])
            dve.wait_ge(x_done, NG)

        @block.scalar
        def _(act):
            def turned(h, b):
                g = 2 * h + b
                act.wait_ge(rows_turned, g + 1)
                after(act, first_done, g - 1)
                nc.scalar.activation(hT[b][:], psH[:], ACT.Relu).then_inc(hT_done, 1)
                act.wait_ge(adj_turned, g + 1)
                after(act, second_done, g - 1)
                after(act, kept, g - 1)
                nc.scalar.activation(aT[b][:], psA[:], ACT.Copy).then_inc(aT_done, 1)

            def products(h, b):
                g = 2 * h + b
                act.wait_ge(first_done, g + 1)
                after(act, second_done, g - 1)
                nc.scalar.activation(u[b][:], ps1[b][:, :, P:2 * P], ACT.Copy).then_inc(u_done, 1)
                act.wait_ge(sums_ready, g + 1)
                nc.scalar.activation(sums[:, bass.ds(g * 2 * GB, 2 * GB)], psS[:, 0:2 * GB], ACT.Copy)\
                  .then_inc(sums_done, 1)

            staggered(act, [(0, turned), (1, products)])
            act.wait_ge(sums_done, NG)

        @block.tensor
        def _(pe):
            def turn(h, b):
                g = 2 * h + b
                pe.wait_ge(rows_ready, g + 1)
                after(pe, hT_done, g)
                for j in range(GB):
                    last = nc.tensor.transpose(psH[:, j, :], hn[b][:, j, :], c["ident"][:])
                last.then_inc(rows_turned, 1)
                after(pe, aT_done, g)
                for j in range(GB):
                    last = nc.tensor.transpose(psA[:, j, :], adj[b][:, j, :], c["ident"][:])
                last.then_inc(adj_turned, 1)

            def first(h, b):
                g = 2 * h + b
                pe.wait_ge(hT_done, g + 1)
                after(pe, bias_done, g - 1)
                for j in range(GB):
                    last = nc.tensor.matmul(ps1[b][:, j, :], hT[b][:, j, :],
                                            wcat[:].rearrange("k t o -> k (t o)"), start=True, stop=True)
                last.then_inc(first_done, 1)
                pe.wait_ge(aT_done, g + 1)
                after(pe, sums_done, g)
                for t, side in enumerate((aT[b], adj[b])):
                    for j in range(GB):
                        last = nc.tensor.matmul(psS[:, t * GB + j:t * GB + j + 1], side[:, j, :], c["ones"][:],
                                                start=True, stop=True)
                last.then_inc(sums_ready, 1)

            def second(h, b):
                g = 2 * h + b
                pe.wait_ge(u_done, g + 1)
                after(pe, gathered, g)
                for j in range(GB):
                    last = nc.tensor.matmul(ps2[:, j, :], aT[b][:, j, :], u[b][:, j, :], start=True, stop=True)
                last.then_inc(second_done, 1)

            pe.wait_ge(w_loaded, 32)
            staggered(pe, [(0, turn), (1, first), (2, second)])


def layer1(nc, c):
    x, pattern, w_hi, w_lo = c["x"], c["pattern"], c["w_hi"], c["w_lo"]
    R_, Z_, N_ = range(GATES)
    with ExitStack() as ctx:
        sb = lambda name, shape, dt=F32: ctx.enter_context(nc.sbuf_tensor(name, shape, dt))
        sem = lambda name: ctx.enter_context(nc.semaphore(name))
        ps = lambda name: ctx.enter_context(nc.psum_tensor(name, [P, W], F32))
        state = [sb(f"state{j}", [P, W]) for j in range(SLOTS)]
        state_hi = [sb(f"state_hi{j}", [P, W], F16) for j in range(SLOTS)]
        state_lo = [sb(f"state_lo{j}", [P, W], F16) for j in range(SLOTS)]
        node_hi = [sb(f"node_hi{b}", [P, W], F16) for b in range(2)]
        node_lo = [sb(f"node_lo{b}", [P, W], F16) for b in range(2)]
        agg_hi = [sb(f"agg_hi{b}", [P, W], F16) for b in range(2)]
        agg_lo = [sb(f"agg_lo{b}", [P, W], F16) for b in range(2)]
        cand = [sb(f"cand{b}", [P, W]) for b in range(2)]
        zgate = [sb(f"zgate{b}", [P, W]) for b in range(2)]
        diff = sb("diff", [P, W])
        rows = sb("rows", [P, W])
        stats = sb("l1_stats", [P, SLOTS, GB, 6])
        mv = sb("l1_mv", [P, SLOTS, GB, 2])
        var = sb("l1_var", [P, SLOTS, GB])
        rstd = sb("l1_rstd", [P, SLOTS, GB])
        psT = [ps(f"psT{b}") for b in range(2)]
        psQ = [ps(f"psQ{b}") for b in range(2)]
        psR, psZ, psI, psH = ps("psR"), ps("psZ"), ps("psI"), ps("psHn")
        (r_ready, z_ready, i_ready, h_ready, r_done, z_done, reset_done, pre_done, n_done, diff_done,
         gated, state_new) = (sem(n) for n in (
             "r_ready z_ready i_ready h_ready r_done z_done reset_done pre_done n_done diff_done "
             "gated state_new").split())
        (turned, node_hi_done, node_ready, agg_ready, agg_hi_done, agg_split, state_hi_done,
         state_ready) = (sem(n) for n in (
             "turned node_hi_done node_ready agg_ready agg_hi_done agg_split state_hi_done state_ready").split())
        (stats_done, moments_done, var_ready, rstd_ready, normed, rows_ready, out_turned, out_done) = (
            sem("l1_" + n) for n in (
                "stats_done moments_done var_ready rstd_ready normed rows_ready out_turned out_done").split())
        block = ctx.enter_context(nc.Block())


        def quads(eng, step):
            for k in range(QUAD):
                step(0, 0, k, True, False)
            with eng.Fori(1, NQ - 1) as q:
                for k in range(QUAD):
                    step(q * QUAD, q * SLOTS, k, False, False)
            for k in range(QUAD):
                step((NQ - 1) * QUAD, (NQ - 1) * SLOTS, k, False, True)

        def ahead(k, by):
            k += by
            return k % QUAD < ROUND, k % ROUND, (k // QUAD) * SLOTS + k % ROUND

        @block.tensor
        def _(pe):
            def gate(bank, gate_at, layer, hi, lo, start, stop):
                w_at = bass.ts(gate_at, P)
                nc.tensor.matmul(bank[:], w_hi[:, layer, w_at], hi, start=start, stop=False)
                nc.tensor.matmul(bank[:], w_hi[:, layer, w_at], lo, start=False, stop=False)
                return nc.tensor.matmul(bank[:], w_lo[:, layer, w_at], hi, start=False, stop=stop)

            def turn(bank, src):
                for j in range(GB):
                    last = nc.tensor.transpose(bank[:, bass.ts(j, P)], src[:, bass.ts(j, P)], c["ident"][:])
                return last

            def enter(s, group, slot):
                pe.wait_ge(rows_ready, group + 1)
                after(pe, node_ready, s)
                after(pe, state_hi_done, s)
                turn(psT[1 - slot % 2], rows).then_inc(turned, 1)

            def leave(s, group, slot):
                pe.wait_ge(state_new, s - SLOTS + 1)
                pe.wait_ge(node_ready, s - 1)
                pe.wait_ge(state_hi_done, s)
                if not (isinstance(group, int) and group <= 0):
                    pe.wait_ge(out_done, group)
                turn(psT[slot % 2], state[slot]).then_inc(out_turned, 1)

            def aggregate(s, group, b):
                pe.wait_ge(node_ready, s + 1)
                after(pe, agg_split, s - 1)
                for j in range(GB):
                    at = bass.ts(j, P)
                    nc.tensor.matmul(psQ[b][:, at], node_hi[b][:, at], cols(pattern, group, j),
                                     start=True, stop=False)
                    last = nc.tensor.matmul(psQ[b][:, at], node_lo[b][:, at], cols(pattern, group, j),
                                            start=False, stop=True)
                last.then_inc(agg_ready, 1)

            def step(s0, g0, k, first, last_quad):
                s = s0 + k
                slot, b, layer = k % ROUND, k % 2, k // ROUND
                hi, lo = state_hi[slot][:], state_lo[slot][:]
                pe.wait_ge(state_ready, s + 1)
                after(pe, reset_done, s)
                gate(psH, N_, LAYERS, hi, lo, True, True).then_inc(h_ready, 1)
                if not (last_quad and k + 2 >= QUAD):
                    new, to, ahead_g = ahead(k, 2)
                    if new:
                        if not (first and k + 2 < QUAD):
                            leave(s + 2, g0 + ahead_g - SLOTS, to)
                        enter(s + 2, g0 + ahead_g, to)
                    else:
                        pe.wait_ge(state_new, s - 1)
                        after(pe, node_ready, s + 1)
                        if k + 2 < ROUND + 2:
                            pe.wait_ge(state_hi_done, s0 + ROUND)
                            if not first:
                                pe.wait_ge(out_done, g0)
                        turn(psT[to % 2], state[to]).then_inc(turned, 1)
                after(pe, r_done, s)
                gate(psR, R_, LAYERS, hi, lo, True, False)
                after(pe, z_done, s)
                gate(psZ, Z_, LAYERS, hi, lo, True, False)
                pe.wait_ge(agg_split, s + 1)
                gate(psR, R_, layer, agg_hi[b][:], agg_lo[b][:], False, True).then_inc(r_ready, 1)
                after(pe, pre_done, s)
                gate(psI, N_, layer, agg_hi[b][:], agg_lo[b][:], True, True).then_inc(i_ready, 1)
                if not (last_quad and k + 1 >= QUAD):
                    _, _, ahead_g = ahead(k, 1)
                    aggregate(s + 1, g0 + ahead_g, 1 - b)
                gate(psZ, Z_, layer, agg_hi[b][:], agg_lo[b][:], False, True).then_inc(z_ready, 1)

            enter(0, 0, 0)
            enter(1, 1, 1)
            aggregate(0, 0, 0)
            quads(pe, step)
            for slot in range(SLOTS):
                group = NG - SLOTS + slot
                pe.wait_ge(state_new, NQ * QUAD - SLOTS + slot + 1)
                pe.wait_ge(node_ready, NQ * QUAD)
                after(pe, out_done, group - 1 if slot >= 2 else NG - SLOTS)
                turn(psT[slot % 2], state[slot]).then_inc(out_turned, 1)

        @block.scalar
        def _(act):
            def enter(s, group, slot):
                act.wait_ge(rows_ready, group + 1)
                after(act, agg_ready, s - 1)
                nc.scalar.activation(node_hi[slot % 2][:], rows[:], ACT.Copy, scale=SH).then_inc(node_hi_done, 1)
                act.wait_ge(turned, s + 1)
                nc.scalar.activation(state[slot][:], psT[1 - slot % 2][:], ACT.Copy)
                nc.scalar.activation(state_hi[slot][:], psT[1 - slot % 2][:], ACT.Copy, scale=SH)\
                  .then_inc(state_hi_done, 1)

            def aggregate_hi(s, b):
                act.wait_ge(agg_ready, s + 1)
                after(act, z_ready, s - 1)
                nc.scalar.activation(agg_hi[b][:], psQ[b][:], ACT.Copy).then_inc(agg_hi_done, 1)

            def step(s0, g0, k, first, last_quad):
                s = s0 + k
                b = k % 2
                if not (last_quad and k + 2 >= QUAD):
                    new, to, ahead_g = ahead(k, 2)
                    if new:
                        enter(s + 2, g0 + ahead_g, to)
                    else:
                        act.wait_ge(turned, s + 3)
                        after(act, agg_ready, s + 1)
                        nc.scalar.activation(node_hi[b][:], psT[b][:], ACT.Copy, scale=SH)\
                          .then_inc(node_hi_done, 1)
                act.wait_ge(r_ready, s + 1)
                after(act, state_new, s - 1)
                nc.scalar.activation(cand[b][:], psR[:], ACT.Sigmoid, bias=c["brz"][:, 0:1],
                                     scale=c["gscale"][:]).then_inc(r_done, 1)
                if 1 <= k <= QUAD - ROUND:
                    act.wait_ge(state_new, s)
                    slot = (k - 1) % ROUND
                    nc.scalar.activation(state_hi[slot][:], state[slot][:], ACT.Copy, scale=SH)\
                      .then_inc(state_hi_done, 1)
                if not (last_quad and k + 1 >= QUAD):
                    aggregate_hi(s + 1, 1 - b)
                act.wait_ge(z_ready, s + 1)
                after(act, gated, s - 1)
                nc.scalar.activation(zgate[b][:], psZ[:], ACT.Sigmoid, bias=c["brz"][:, 1:2],
                                     scale=c["gscale"][:]).then_inc(z_done, 1)
                act.wait_ge(pre_done, s + 1)
                nc.scalar.activation(cand[b][:], cand[b][:], ACT.Tanh, bias=c["bin"][:],
                                     scale=c["gscale"][:]).then_inc(n_done, 1)

            enter(0, 0, 0)
            enter(1, 1, 1)
            aggregate_hi(0, 0)
            quads(act, step)

        @block.gpsimd
        def _(pool):
            def root(slot, nth):
                pool.wait_ge(var_ready, nth)
                nc.gpsimd.tensor_tensor(rstd[:, slot, :], var[:, slot, :], c["minus_half"][:], ALU.pow)\
                  .then_inc(rstd_ready, 1)

            def step(s0, g0, k, first, last_quad):
                s = s0 + k
                slot, b = k % ROUND, k % 2
                if 2 * ROUND <= k < 3 * ROUND and not last_quad:
                    root(slot, g0 + SLOTS + slot + 1)
                pool.wait_ge(n_done, s + 1)
                after(pool, state_new, s)
                nc.gpsimd.tensor_tensor(diff[:], state[slot][:], cand[b][:], ALU.subtract).then_inc(diff_done, 1)
                pool.wait_ge(diff_done, s + 1)
                pool.wait_ge(z_done, s + 1)
                nc.gpsimd.tensor_tensor(diff[:], diff[:], zgate[b][:], ALU.mult).then_inc(gated, 1)

            for slot in range(SLOTS):
                root(slot, slot + 1)
            quads(pool, step)

        @block.vector
        def _(dve):
            def statistics(slot, group):
                norm_statistics(nc, dve, lambda j: cols(x, group, j), stats[:, slot], mv[:, slot],
                                var[:, slot, :], stats_done, moments_done, var_ready, group + 1)

            def make_rows(s, group, slot):
                dve.wait_ge(rstd_ready, group + 1)
                after(dve, turned, s)
                after(dve, node_hi_done, s)
                after(dve, node_ready, s)
                for j in range(GB):
                    last = nc.vector.tensor_scalar(rows[:, bass.ts(j, P)], cols(x, group, j),
                                                   mv[:, slot, j, 0:1], rstd[:, slot, j:j + 1],
                                                   ALU.subtract, ALU.mult)
                last.then_inc(normed, 1)
                dve.wait_ge(normed, group + 1)
                nc.vector.tensor_scalar(rows[:], rows[:], 0.0, None, ALU.max).then_inc(rows_ready, 1)

            def node_low(s, b, src):
                dve.wait_ge(node_hi_done, s + 1)
                nc.vector.scalar_tensor_tensor(node_lo[b][:], src, SH, node_hi[b][:], ALU.mult, ALU.subtract)\
                  .then_inc(node_ready, 1)

            def state_low(s, slot):
                dve.wait_ge(state_hi_done, s + 1)
                nc.vector.scalar_tensor_tensor(state_lo[slot][:], state[slot][:], SH, state_hi[slot][:],
                                               ALU.mult, ALU.subtract).then_inc(state_ready, 1)

            def aggregate_low(s, b):
                dve.wait_ge(agg_hi_done, s + 1)
                nc.vector.tensor_tensor(agg_lo[b][:], psQ[b][:], agg_hi[b][:], ALU.subtract).then_inc(agg_split, 1)

            def leave(group, slot):
                dve.wait_ge(out_turned, group + 1)
                for j in range(GB):
                    last = nc.vector.scalar_tensor_tensor(
                        cols(x, group, j), psT[slot % 2][:, bass.ts(j, P)],
                        c["mask"][:, bass.ds(group * GB + j, 1)], cols(x, group, j), ALU.mult, ALU.add)
                last.then_inc(out_done, 1)

            def update(s, slot, b):
                dve.wait_ge(gated, s + 1)
                nc.vector.tensor_tensor(state[slot][:], cand[b][:], diff[:], ALU.add).then_inc(state_new, 1)

            def step(s0, g0, k, first, last_quad):
                s = s0 + k
                b = k % 2
                if not (last_quad and k + 2 >= QUAD):
                    new, to, ahead_g = ahead(k, 2)
                    if new:
                        node_low(s + 2, to % 2, rows[:])
                        if not (first and k + 2 < QUAD):
                            leave(g0 + ahead_g - SLOTS, to)
                        state_low(s + 2, to)
                    else:
                        node_low(s + 2, b, psT[b][:])
                if not (first and k == 0):
                    update(s - 1, (k - 1) % ROUND, 1 - b)
                dve.wait_ge(r_done, s + 1)
                dve.wait_ge(h_ready, s + 1)
                nc.vector.scalar_tensor_tensor(cand[b][:], psH[:], c["bhn"][:], cand[b][:], ALU.add, ALU.mult)\
                  .then_inc(reset_done, 1)
                dve.wait_ge(reset_done, s + 1)
                dve.wait_ge(i_ready, s + 1)
                nc.vector.tensor_tensor(cand[b][:], cand[b][:], psI[:], ALU.add).then_inc(pre_done, 1)
                if not (last_quad and k + 1 >= QUAD):
                    aggregate_low(s + 1, 1 - b)
                if 1 <= k <= QUAD - ROUND:
                    state_low(s + 3, (k - 1) % ROUND)
                if ROUND <= k < 2 * ROUND and not last_quad:
                    statistics(k % ROUND, g0 + SLOTS + k % ROUND)
                if not (last_quad and k + 3 >= QUAD):
                    new, to, ahead_g = ahead(k, 3)
                    if new:
                        make_rows(s + 3, g0 + ahead_g, to)

            for slot in range(SLOTS):
                statistics(slot, slot)
            for s in range(2):
                make_rows(s, s, s)
                node_low(s, s, rows[:])
                state_low(s, s)
            make_rows(2, 2, 2)
            aggregate_low(0, 0)
            quads(dve, step)
            update(NQ * QUAD - 1, SLOTS - 1, 1)
            for slot in range(SLOTS):
                leave(NG - SLOTS + slot, slot)
            dve.wait_ge(out_done, NG)


def layer2(nc, c):
    x, adjT, sums = c["x"], c["adjT"], c["sums"]
    with ExitStack() as ctx:
        sb = lambda name, shape, dt=F32: ctx.enter_context(nc.sbuf_tensor(name, shape, dt))
        sem = lambda name: ctx.enter_context(nc.semaphore(name))
        pair = lambda name, shape, dt=F32: [sb(f"{name}{b}", shape, dt) for b in range(2)]
        ps = lambda name, shape: ctx.enter_context(nc.psum_tensor(name, shape, F32))
        wcat = sb("l2_wcat", [P, 2, P])
        gb = sb("l2_gb", [P, 2])
        zero = sb("l2_zero", [P, NG * 2 * GB])
        power = sb("l2_power", [P, NG * 2 * GB])
        rows = pair("l2_rows", [P, GB, P])
        xn = pair("l2_xn", [P, GB, P])
        aS = pair("l2_aS", [P, GB, P])
        xnT = pair("l2_xnT", [P, GB, P])
        u = pair("l2_u", [P, GB, P])
        pre = pair("l2_pre", [P, GB, P])
        soft = pair("l2_soft", [P, GB, P])
        stats = pair("l2_stats", [P, GB, 6])
        mv = pair("l2_mv", [P, GB, 2])
        var = pair("l2_var", [P, GB])
        rstd = pair("l2_rstd", [P, GB])
        stats2 = pair("l2_stats2", [P, GB, 6])
        mv2 = pair("l2_mv2", [P, GB, 2])
        var2 = pair("l2_var2", [P, GB])
        rstd2 = pair("l2_rstd2", [P, GB])
        psX = [ps(f"l2_psX{b}", [P, GB, P]) for b in range(2)]
        ps1 = [ps(f"l2_ps1{b}", [P, GB, 2 * P]) for b in range(2)]
        ps2 = [ps(f"l2_ps2{b}", [P, GB, P]) for b in range(2)]
        (w_loaded, w_link, w_ready, sums_safe, powered, stats_done, moments_done, var_ready, rstd_ready, normed,
         rows_done, stats2_done, moments2_done, var2_ready, rstd2_ready, xn_ready, aS_ready, xn_turned, xnT_done,
         first_done, products_done, second_done, pre_done, low_done, exp_done, log_done, soft_done,
         x_done) = (
            sem("l2_" + n) for n in (
                "w_loaded w_link w_ready sums_safe powered stats_done moments_done var_ready rstd_ready normed "
                "rows_done stats2_done moments2_done var2_ready rstd2_ready xn_ready aS_ready xn_turned xnT_done "
                "first_done products_done second_done pre_done low_done exp_done log_done soft_done "
                "x_done").split())
        block = ctx.enter_context(nc.Block())

        @block.sync
        def _(sp):
            sp.dma_start(wcat[:, 0, :], c["l2_ws_in"]).then_inc(w_loaded, 16)
            sp.dma_start(wcat[:, 1, :], c["l2_wn_in"]).then_inc(w_loaded, 16)
            sp.dma_start(gb[:], c["l2_gb_in"]).then_inc(w_loaded, 16)

        @block.gpsimd
        def _(pool):
            def root(h, b):
                pool.wait_ge(var_ready, 2 * h + b + 1)
                nc.gpsimd.tensor_tensor(rstd[b][:], var[b][:], c["minus_half"][:], ALU.pow).then_inc(rstd_ready, 1)

            def root2(h, b):
                pool.wait_ge(var2_ready, 2 * h + b + 1)
                nc.gpsimd.tensor_tensor(rstd2[b][:], var2[b][:], c["minus_half"][:], ALU.pow)\
                  .then_inc(rstd2_ready, 1)

            def add(h, b):
                g = 2 * h + b
                pool.wait_ge(soft_done, g + 1)
                nc.gpsimd.tensor_tensor(graphs(cols(x, g)), graphs(cols(x, g)), soft[b][:], ALU.add)\
                  .then_inc(x_done, 1)

            pool.wait_ge(sums_safe, 2)
            nc.gpsimd.tensor_tensor(sums[:], sums[:], power[:], ALU.pow).then_inc(powered, 1)
            staggered(pool, [(6, add), (1, root2), (0, root)])
            pool.wait_ge(x_done, NG)

        @block.vector
        def _(dve):
            def front(h, b):
                g = 2 * h + b
                norm_statistics(nc, dve, lambda j: cols(x, g, j), stats[b], mv[b], var[b][:],
                                stats_done, moments_done, var_ready, g + 1)

            def again(h, b):
                g = 2 * h + b
                dve.wait_ge(rstd_ready, g + 1)
                for j in range(GB):
                    last = nc.vector.tensor_scalar(rows[b][:, j, :], cols(x, g, j), mv[b][:, j, 0:1],
                                                   rstd[b][:, j:j + 1], ALU.subtract, ALU.mult)
                last.then_inc(normed, 1)
                dve.wait_ge(normed, g + 1)
                nc.vector.tensor_scalar(rows[b][:], rows[b][:], 0.0, None, ALU.max).then_inc(rows_done, 1)
                dve.wait_ge(rows_done, g + 1)
                norm_statistics(nc, dve, lambda j: rows[b][:, j, :], stats2[b], mv2[b], var2[b][:],
                                stats2_done, moments2_done, var2_ready, g + 1)

            def norm(h, b):
                g = 2 * h + b
                dve.wait_ge(rstd2_ready, g + 1)
                after(dve, xn_turned, g - 1)
                for j in range(GB):
                    last = nc.vector.tensor_scalar(xn[b][:, j, :], rows[b][:, j, :], mv2[b][:, j, 0:1],
                                                   rstd2[b][:, j:j + 1], ALU.subtract, ALU.mult)
                last.then_inc(xn_ready, 1)
                after(dve, second_done, g - 1)
                for j in range(GB):
                    last = nc.vector.tensor_scalar(aS[b][:, j, :], cols(adjT, g, j),
                                                   sums[:, bass.ds(g * 2 * GB + j, 1)], None, ALU.mult)
                last.then_inc(aS_ready, 1)

            def outer(h, b):
                g = 2 * h + b
                dve.wait_ge(second_done, g + 1)
                dve.wait_ge(products_done, g + 1)
                for j in range(GB):
                    last = nc.vector.scalar_tensor_tensor(pre[b][:, j, :], ps2[b][:, j, :],
                                                          sums[:, bass.ds(g * 2 * GB + GB + j, 1)],
                                                          pre[b][:, j, :], ALU.mult, ALU.add)
                last.then_inc(pre_done, 1)
                dve.wait_ge(pre_done, g + 1)
                after(dve, x_done, g - 1)
                nc.vector.scalar_tensor_tensor(soft[b][:].rearrange("p b d -> p (b d)"),
                                               pre[b][:].rearrange("p b d -> p (b d)"), -1.0,
                                               pre[b][:].rearrange("p b d -> p (b d)"),
                                               ALU.mult, ALU.min).then_inc(low_done, 1)

            def finish(h, b):
                g = 2 * h + b
                dve.wait_ge(log_done, g + 1)
                nc.vector.scalar_tensor_tensor(soft[b][:].rearrange("p b d -> p (b d)"),
                                               pre[b][:].rearrange("p b d -> p (b d)"), 0.0,
                                               soft[b][:].rearrange("p b d -> p (b d)"),
                                               ALU.max, ALU.add).then_inc(soft_done, 1)

            dve.wait_ge(w_loaded, 48)
            nc.vector.tensor_tensor(wcat[:, 0, :], wcat[:, 0, :], wcat[:, 1, :], ALU.add).then_inc(w_ready, 1)
            nc.vector.memset(power[:], -0.5).then_inc(sums_safe, 1)
            nc.vector.tensor_scalar(zero[:], sums[:], 0.0, None, ALU.is_equal).then_inc(w_link, 1)
            dve.wait_ge(w_link, 1)
            nc.vector.tensor_tensor(sums[:], sums[:], zero[:], ALU.add).then_inc(sums_safe, 1)
            nc.vector.tensor_scalar(zero[:], zero[:], -1.0, 1.0, ALU.mult, ALU.add).then_inc(w_link, 1)
            dve.wait_ge(powered, 1)
            dve.wait_ge(w_link, 2)
            nc.vector.tensor_tensor(sums[:], sums[:], zero[:], ALU.mult).then_inc(w_link, 1)
            dve.wait_ge(w_link, 3)
            outer_part = sums[:].rearrange("p (g t j) -> p g t j", t=2, j=GB)[:, :, 1, :]
            nc.vector.tensor_scalar(outer_part, outer_part, -1.0, None, ALU.mult).then_inc(w_link, 1)
            dve.wait_ge(w_link, 4)
            staggered(dve, [(5, finish), (4, outer), (2, norm), (1, again), (0, front)])

        @block.scalar
        def _(act):
            def turned(h, b):
                g = 2 * h + b
                act.wait_ge(xn_turned, g + 1)
                after(act, first_done, g - 1)
                nc.scalar.activation(xnT[b][:], psX[b][:], ACT.Identity, bias=gb[:, 1:2], scale=gb[:, 0:1])\
                  .then_inc(xnT_done, 1)

            def products(h, b):
                g = 2 * h + b
                act.wait_ge(first_done, g + 1)
                after(act, second_done, g - 1)
                nc.scalar.activation(u[b][:], ps1[b][:, :, P:2 * P], ACT.Copy)
                after(act, soft_done, g - 1)
                nc.scalar.activation(pre[b][:], ps1[b][:, :, 0:P], ACT.Copy).then_inc(products_done, 1)

            def soften(h, b):
                g = 2 * h + b
                act.wait_ge(low_done, g + 1)
                nc.scalar.activation(soft[b][:], soft[b][:], ACT.Exp).then_inc(exp_done, 1)
                act.wait_ge(exp_done, g + 1)
                nc.scalar.activation(soft[b][:], soft[b][:], ACT.Ln, bias=1.0).then_inc(log_done, 1)

            act.wait_ge(w_loaded, 48)
            staggered(act, [(3, soften), (0, turned), (1, products)])

        @block.tensor
        def _(pe):
            def turn(h, b):
                g = 2 * h + b
                pe.wait_ge(xn_ready, g + 1)
                after(pe, xnT_done, g - 1)
                for j in range(GB):
                    last = nc.tensor.transpose(psX[b][:, j, :], xn[b][:, j, :], c["ident"][:])
                last.then_inc(xn_turned, 1)

            def first(h, b):
                g = 2 * h + b
                pe.wait_ge(xnT_done, g + 1)
                after(pe, products_done, g - 1)
                for j in range(GB):
                    last = nc.tensor.matmul(ps1[b][:, j, :], xnT[b][:, j, :],
                                            wcat[:].rearrange("k t o -> k (t o)"), start=True, stop=True)
                last.then_inc(first_done, 1)

            def second(h, b):
                g = 2 * h + b
                pe.wait_ge(products_done, g + 1)
                pe.wait_ge(aS_ready, g + 1)
                after(pe, pre_done, g - 1)
                for j in range(GB):
                    last = nc.tensor.matmul(ps2[b][:, j, :], aS[b][:, j, :], u[b][:, j, :], start=True, stop=True)
                last.then_inc(second_done, 1)

            pe.wait_ge(w_ready, 1)
            staggered(pe, [(2, second), (1, first), (0, turn)])


def layer3(nc, c):
    x, adjT = c["x"], c["adjT"]
    HID = 2
    with ExitStack() as ctx:
        sb = lambda name, shape, dt=F32: ctx.enter_context(nc.sbuf_tensor(name, shape, dt))
        sem = lambda name: ctx.enter_context(nc.semaphore(name))
        pair = lambda name, shape, dt=F32: [sb(f"{name}{b}", shape, dt) for b in range(2)]
        ps = lambda name, shape: ctx.enter_context(nc.psum_tensor(name, shape, F32))
        w1 = sb("l3_w1", [P, HID, P])
        w2 = sb("l3_w2", [P, HID, P])
        b1 = sb("l3_b1", [P, HID])
        b2 = sb("l3_b2", [P, GB, P])
        eps1 = sb("l3_eps1", [P, 1])
        self_loop = sb("l3_self_loop", [P, GB, P])
        rows = pair("l3_rows", [P, GB, P])
        aI = pair("l3_aI", [P, GB, P])
        gT = pair("l3_gT", [P, W])
        hid = pair("l3_hid", [P, HID, W])
        out = pair("l3_out", [P, GB, P])
        stats = pair("l3_stats", [P, GB, 6])
        mv = pair("l3_mv", [P, GB, 2])
        var = pair("l3_var", [P, GB])
        rstd = pair("l3_rstd", [P, GB])
        psG = [ps(f"l3_psG{b}", [P, W]) for b in range(2)]
        psA = [ps(f"l3_psA{b}", [P, HID, W]) for b in range(2)]
        psO = [ps(f"l3_psO{b}", [P, GB, P]) for b in range(2)]
        stored = [sem(f"l3_stored{b}") for b in range(2)]
        (w_loaded, eps_ready, loop_ready, stats_done, moments_done, var_ready, rstd_ready, normed, rows_ready,
         aI_ready, mixed, gT_done, hidden, hid_done, projected, summed, out_ready) = (
            sem("l3_" + n) for n in (
                "w_loaded eps_ready loop_ready stats_done moments_done var_ready rstd_ready normed rows_ready "
                "aI_ready mixed gT_done hidden hid_done projected summed out_ready").split())
        block = ctx.enter_context(nc.Block())

        @block.sync
        def _(sp):
            for dst, src in ((w1[:], c["l3_w1_in"].rearrange("k (t o) -> k t o", t=HID)),
                             (w2[:], c["l3_w2_in"].rearrange("(t k) o -> k t o", t=HID)),
                             (b1[:], c["l3_b1_in"]), (b2[:], c["l3_b2_in"].rearrange("p (b d) -> p b d", b=GB)),
                             (eps1[:], c["l3_eps_in"])):
                sp.dma_start(dst, src).then_inc(w_loaded, 16)

            def store(h, b):
                g = 2 * h + b
                sp.wait_ge(out_ready, g + 1)
                sp.dma_start(c["out"][bass.ts(g, GB)].rearrange("b n d -> n b d"), out[b][:])\
                  .then_inc(stored[b], 16)

            staggered(sp, [(0, store)])
            for b in range(2):
                sp.wait_ge(stored[b], 16 * (NG // 2))

        @block.gpsimd
        def _(pool):
            def root(h, b):
                pool.wait_ge(var_ready, 2 * h + b + 1)
                nc.gpsimd.tensor_tensor(rstd[b][:], var[b][:], c["minus_half"][:], ALU.pow).then_inc(rstd_ready, 1)

            def loops(h, b):
                g = 2 * h + b
                after(pool, mixed, g - 1)
                nc.gpsimd.tensor_tensor(aI[b][:], graphs(cols(adjT, g)), self_loop[:], ALU.add)\
                  .then_inc(aI_ready, 1)

            def bias(h, b):
                g = 2 * h + b
                pool.wait_ge(summed, g + 1)
                nc.gpsimd.tensor_tensor(out[b][:], out[b][:], b2[:], ALU.add).then_inc(out_ready, 1)

            pool.wait_ge(loop_ready, GB)
            staggered(pool, [(5, bias), (1, loops), (0, root)])

        @block.vector
        def _(dve):
            def front(h, b):
                g = 2 * h + b
                norm_statistics(nc, dve, lambda j: cols(x, g, j), stats[b], mv[b], var[b][:],
                                stats_done, moments_done, var_ready, g + 1)

            def norm(h, b):
                g = 2 * h + b
                dve.wait_ge(rstd_ready, g + 1)
                after(dve, mixed, g - 1)
                for j in range(GB):
                    last = nc.vector.tensor_scalar(rows[b][:, j, :], cols(x, g, j), mv[b][:, j, 0:1],
                                                   rstd[b][:, j:j + 1], ALU.subtract, ALU.mult)
                last.then_inc(normed, 1)
                dve.wait_ge(normed, g + 1)
                nc.vector.tensor_scalar(rows[b][:], rows[b][:], 0.0, None, ALU.max).then_inc(rows_ready, 1)

            def finish(h, b):
                g = 2 * h + b
                dve.wait_ge(projected, g + 1)
                after(dve, stored[b], 16 * h)
                nc.vector.tensor_tensor(out[b][:], psO[b][:], graphs(cols(x, g)), ALU.add).then_inc(summed, 1)

            dve.wait_ge(w_loaded, 5 * 16)
            nc.vector.tensor_scalar(eps1[:], eps1[:], 1.0, None, ALU.add).then_inc(eps_ready, 1)
            dve.wait_ge(eps_ready, 1)
            for j in range(GB):
                nc.vector.tensor_scalar(self_loop[:, j, :], c["ident"][:], eps1[:], None, ALU.mult)\
                  .then_inc(loop_ready, 1)
            staggered(dve, [(4, finish), (1, norm), (0, front)])

        @block.scalar
        def _(act):
            def mixed_rows(h, b):
                g = 2 * h + b
                act.wait_ge(mixed, g + 1)
                after(act, hidden, g - 1)
                nc.scalar.activation(gT[b][:], psG[b][:], ACT.Copy).then_inc(gT_done, 1)

            def hidden_rows(h, b):
                g = 2 * h + b
                act.wait_ge(hidden, g + 1)
                after(act, projected, g - 1)
                for t in range(HID):
                    last = nc.scalar.activation(hid[b][:, t, :], psA[b][:, t, :], ACT.Relu, bias=b1[:, t:t + 1])
                last.then_inc(hid_done, 1)

            act.wait_ge(w_loaded, 5 * 16)
            staggered(act, [(0, mixed_rows), (1, hidden_rows)])

        @block.tensor
        def _(pe):
            def mix(h, b):
                g = 2 * h + b
                pe.wait_ge(rows_ready, g + 1)
                pe.wait_ge(aI_ready, g + 1)
                after(pe, gT_done, g - 1)
                for j in range(GB):
                    last = nc.tensor.matmul(psG[b][:, bass.ts(j, P)], rows[b][:, j, :], aI[b][:, j, :],
                                            start=True, stop=True)
                last.then_inc(mixed, 1)

            def hide(h, b):
                g = 2 * h + b
                pe.wait_ge(gT_done, g + 1)
                after(pe, hid_done, g - 1)
                for t in range(HID):
                    last = nc.tensor.matmul(psA[b][:, t, :], w1[:, t, :], gT[b][:], start=True, stop=True)
                last.then_inc(hidden, 1)

            def project(h, b):
                g = 2 * h + b
                pe.wait_ge(hid_done, g + 1)
                after(pe, summed, g - 1)
                for j in range(GB):
                    for t in range(HID):
                        last = nc.tensor.matmul(psO[b][:, j, :], hid[b][:, t, bass.ts(j, P)], w2[:, t, :],
                                                start=(t == 0), stop=(t == HID - 1))
                last.then_inc(projected, 1)

            pe.wait_ge(w_loaded, 5 * 16)
            staggered(pe, [(0, mix), (1, hide), (2, project)])


def gnn_stack_kernel(nc, c):
    with ExitStack() as ctx:
        sb = lambda name, shape, dt=F32: ctx.enter_context(nc.sbuf_tensor(name, shape, dt))
        c["x"] = sb("x", [P, NG * W])
        c["adjT"] = sb("adjT", [P, NG * W])
        c["pattern"] = sb("pattern", [P, NG * W], F16)
        c["sums"] = sb("sums", [P, NG * 2 * GB])
        c["w_hi"] = sb("w_hi", [P, LAYERS + 1, GATES * P], F16)
        c["w_lo"] = sb("w_lo", [P, LAYERS + 1, GATES * P], F16)
        c["ident"] = sb("ident", [P, P])
        c["ones"] = sb("ones", [P, 1])
        c["minus_half"] = sb("minus_half", [P, GB])
        c["mask"] = sb("mask", [P, GRAPHS])
        c["gscale"] = sb("gscale", [P, 1])
        c["bhn"] = sb("bhn", [P, 1])
        c["brz"] = sb("brz", [P, 2])
        c["bin"] = sb("bin", [P, 1])
        prepare(nc, c)
        layer0(nc, c)
        layer1(nc, c)
        layer2(nc, c)
        layer3(nc, c)


def kernel(**inputs):
    import numpy as np
    import concourse.bacc as bacc
    from concourse.bass_utils import run_bass_kernel_spmd

    a = {k: np.asarray(v) for k, v in inputs.items()}
    column = lambda v, n: np.ascontiguousarray(v.reshape(n, P).T)
    spread = lambda v: np.ascontiguousarray(np.broadcast_to(np.tile(v, GB), (P, W)))
    arrays = {
        "x_in": a["x"], "adj_in": a["adj"],
        "mask_in": np.ascontiguousarray(a["nodemask"].T),
        "l0_w_in": a["L0_gnn_weight"], "l0_b_in": spread(a["L0_gnn_bias"]),
        "msgT_in": np.ascontiguousarray(a["L1_gnn_weight"].transpose(0, 2, 1)),
        "ihT_in": np.ascontiguousarray(a["L1_gnn_w_ih"].T), "hhT_in": np.ascontiguousarray(a["L1_gnn_w_hh"].T),
        "bih_in": column(a["L1_gnn_b_ih"], GATES), "bhh_in": column(a["L1_gnn_b_hh"], GATES),
        "l2_ws_in": a["L2_gnn_W_self"], "l2_wn_in": a["L2_gnn_W_neigh"],
        "l2_gb_in": np.ascontiguousarray(np.stack([a["L2_gnn_gamma"], a["L2_gnn_beta"]], axis=1)),
        "l3_w1_in": a["L3_gnn_W1"], "l3_b1_in": column(a["L3_gnn_b1"], 2),
        "l3_w2_in": a["L3_gnn_W2"], "l3_b2_in": spread(a["L3_gnn_b2"]),
        "l3_eps_in": np.ascontiguousarray(np.broadcast_to(a["L3_gnn_eps"], (P, 1))),
    }
    nc = bacc.Bacc("TRN2", target_bir_lowering=False, num_devices=1)
    c = {n: nc.dram_tensor(n, v.shape, mybir.dt.from_np(v.dtype), kind="ExternalInput").ap()
         for n, v in arrays.items()}
    c["out"] = nc.dram_tensor("out", (GRAPHS, P, P), F32, kind="ExternalOutput").ap()
    gnn_stack_kernel(nc, c)
    r = run_bass_kernel_spmd(nc, [arrays], core_ids=[0])
    return r.results[0]["out"]
```

```python
from contextlib import ExitStack

import concourse.bass as bass
from concourse import mybir
from concourse.alu_op_type import AluOpType as ALU

F32 = mybir.dt.float32
F16 = mybir.dt.float16
I32 = mybir.dt.int32
ACT = mybir.ActivationFunctionType
AX = mybir.AxisListType.X

P = 128
GRAPHS = 128
GB = 4
RING = 4
NG = GRAPHS // GB
W = GB * P
LAYERS = 5
GATES = 3
LN_EPS = 1e-5
ROW_EPS = 1e-8
SH = 32.0
SW = 256.0
SLOTS = 4
QUAD = LAYERS * SLOTS
STAGGER = QUAD // SLOTS
EMPTY = sum(STAGGER * j // SLOTS for j in range(SLOTS))
RAW_AHEAD, MOMENTS_AHEAD, ROOT_AHEAD, CENTRE_AHEAD, ROWS_AHEAD = 9, 8, 7, 6, 5
NQ = NG // SLOTS


def after(eng, sem, value):
    if not (isinstance(value, int) and value <= 0):
        eng.wait_ge(sem, value)


def staggered(eng, stages):
    head = max(lag for lag, _ in stages) + RING
    head += -head % RING

    def plain(t):
        for lag, stage in stages:
            if 0 <= t - lag < NG:
                stage((t - lag) // RING, (t - lag) % RING)

    for t in range(head):
        plain(t)
    with eng.Fori(0, (NG - head) // RING) as i:
        for u in range(RING):
            for lag, stage in stages:
                k = head + u - lag
                stage(i + k // RING, k % RING)
    for t in range(NG, NG + head - RING):
        plain(t)


def dma_count(q, b, back):
    return (b - back) % RING, 16 * (q + (b - back) // RING + 1)


def cols(tile, g, j=None):
    return tile[:, bass.ds(g * W, W)] if j is None else tile[:, bass.ds(g * W + j * P, P)]


def graphs(ap):
    return ap.rearrange("p (b d) -> p b d", b=GB)


def prepare(nc, c):
    with ExitStack() as ctx:
        sb = lambda name, shape, dt=F32: ctx.enter_context(nc.sbuf_tensor(name, shape, dt))
        sem = lambda name: ctx.enter_context(nc.semaphore(name))
        msgT = sb("msgT", [P, LAYERS, P])
        ihT = sb("ihT", [P, GATES * P])
        wide = sb("wide", [P, LAYERS + 1, GATES * P])
        ext = sb("ext", [P, 2])
        ext_all = sb("ext_all", [P, 2])
        top = sb("top", [P, 4])
        wscale = sb("wscale", [P, 1])
        bih = sb("bih", [P, GATES])
        bhh = sb("bhh", [P, GATES])
        fold = [ctx.enter_context(nc.psum_tensor(f"fold{l}", [P, W], F32)) for l in range(LAYERS)]
        loaded, ident0, folded = sem("w_loaded"), sem("ident0"), sem("folded")
        ident_ok, copied, extremes, spread = sem("ident_ok"), sem("copied"), sem("extremes"), sem("spread")
        link, done = sem("w_link"), sem("w_done")
        block = ctx.enter_context(nc.Block())

        @block.sync
        def _(sp):
            for dst, src in ((msgT[:], c["msgT_in"].rearrange("l k c -> k l c")), (ihT[:], c["ihT_in"]),
                             (wide[:, LAYERS, :], c["hhT_in"]), (bih[:], c["bih_in"]), (bhh[:], c["bhh_in"]),
                             (c["mask"][:], c["mask_in"])):
                sp.dma_start(dst, src).then_inc(loaded, 16)

        @block.gpsimd
        def _(pool):
            nc.gpsimd.memset(c["ident"][:], 0.0).then_inc(ident0, 1)
            pool.wait_ge(ident0, 1)
            nc.gpsimd.affine_select(out=c["ident"][:], in_=c["ident"][:], compare_op=ALU.not_equal, fill=1.0,
                                    base=0, pattern=[[-1, P]], channel_multiplier=1).then_inc(ident_ok, 1)
            pool.wait_ge(extremes, 2)
            nc.gpsimd.partition_all_reduce(ext_all[:], ext[:], P,
                                           bass.bass_isa.ReduceOp.absmax).then_inc(spread, 1)

        @block.tensor
        def _(pe):
            pe.wait_ge(loaded, 6 * 16)
            for l in range(LAYERS):
                nc.tensor.matmul(fold[l][:, 0:GATES * P], msgT[:, l, :], ihT[:], start=True, stop=True)\
                  .then_inc(folded, 1)

        @block.vector
        def _(dve):
            count = [0]

            def linked(ins):
                count[0] += 1
                ins.then_inc(link, 1)
                dve.wait_ge(link, count[0])

            nc.vector.memset(c["minus_half"][:], -0.5)
            nc.vector.memset(c["ones"][:], 1.0)
            dve.wait_ge(loaded, 6 * 16)
            for l in range(LAYERS):
                dve.wait_ge(folded, l + 1)
                last = nc.vector.tensor_copy(wide[:, l, :], fold[l][:, 0:GATES * P])
            linked(last)
            flat = wide[:].rearrange("p l e -> p (l e)")
            nc.vector.tensor_reduce(ext[:, 0:1], flat, AX, ALU.max).then_inc(extremes, 1)
            nc.vector.tensor_reduce(ext[:, 1:2], flat, AX, ALU.min).then_inc(extremes, 1)
            dve.wait_ge(spread, 1)
            linked(nc.vector.tensor_tensor(top[:, 1:2], ext_all[:, 0:1], ext_all[:, 1:2], ALU.max))
            linked(nc.vector.tensor_scalar(top[:, 2:3].bitcast(I32), top[:, 1:2].bitcast(I32), 0x7F800000, None,
                                           ALU.bitwise_and))
            linked(nc.vector.tensor_scalar(top[:, 0:1], top[:, 2:3], 2.0 ** -60, None, ALU.max))
            linked(nc.vector.reciprocal(top[:, 3:4], top[:, 0:1]))
            linked(nc.vector.tensor_scalar(wscale[:], top[:, 3:4], SW, None, ALU.mult))
            nc.vector.tensor_scalar(c["gscale"][:], top[:, 0:1], 1.0 / (SW * SH), None, ALU.mult)
            nc.vector.tensor_scalar(c["bhn"][:], bhh[:, 2:3], wscale[:], SH, ALU.mult, ALU.mult)
            nc.vector.tensor_tensor(c["brz"][:], bih[:, 0:2], bhh[:, 0:2], ALU.add)
            nc.vector.tensor_copy(c["bin"][:], bih[:, 2:3])
            hi, lo = (c[n][:].rearrange("p l e -> p (l e)") for n in ("w_hi", "w_lo"))
            linked(nc.vector.tensor_scalar(hi, flat, wscale[:], None, ALU.mult))
            nc.vector.scalar_tensor_tensor(lo, flat, wscale[:], hi, ALU.mult, ALU.subtract).then_inc(done, 1)
            dve.wait_ge(done, 1)


def statistics(nc, dve, x_of, stats, stats_done, mv, moments_done, var, var_ready, nth):
    def raw():
        for j in range(GB):
            last = nc.vector.bn_stats(stats[:, j, :], x_of(j))
        last.then_inc(stats_done, 1)

    def moments():
        dve.wait_ge(stats_done, nth)
        nc.vector.nop(nofuse=True)
        for j in range(GB):
            last = nc.vector.bn_aggr(mv[:, j, :], stats[:, j, :])
        last.then_inc(moments_done, 1)

    def variance():
        dve.wait_ge(moments_done, nth)
        nc.vector.tensor_scalar(var, mv[:, :, 1], LN_EPS, None, ALU.add).then_inc(var_ready, 1)

    return raw, moments, variance


def per_node(ap):
    return ap.to_broadcast([P, GB, P])


def layer0(nc, c):
    x, adjT, pattern, sums = c["x"], c["adjT"], c["pattern"], c["sums"]
    with ExitStack() as ctx:
        sb = lambda name, shape, dt=F32: ctx.enter_context(nc.sbuf_tensor(name, shape, dt))
        sem = lambda name: ctx.enter_context(nc.semaphore(name))
        ring = lambda name, n, shape, dt=F32: [sb(f"l0_{name}{b}", shape, dt) for b in range(n)]
        ps = lambda name, shape: ctx.enter_context(nc.psum_tensor(name, shape, F32))
        wcat = sb("l0_wcat", [P, 2, P])
        bias = sb("l0_bias", [P, GB, P])
        adj = ring("adj", RING, [P, GB, P])
        hn = ring("hn", RING, [P, GB, P])
        hT = ring("hT", 2, [P, GB, P])
        aT = ring("aT", 2, [P, GB, P])
        u = ring("u", 2, [P, GB, P + 1])
        pre = ring("pre", 2, [P, GB, P])
        stats = ring("stats", 2, [P, GB, 6])
        mv = ring("mv", 2, [P, GB, 2])
        var = ring("var", 2, [P, GB])
        rstd = ring("rstd", RING, [P, GB])
        rinv = ring("rinv", 2, [P, GB])
        psA, psH = ps("l0_psA", [P, GB, P]), ps("l0_psH", [P, GB, P])
        ps1 = ps("l0_ps1", [P, GB, 2 * P])
        ps2 = [ps(f"l0_ps2{b}", [P, 2, W]) for b in range(2)]
        of_graph = lambda b, j: ps2[b % 2][:, j // 2, bass.ds(j % 2 * (P + 1), P + 1)]
        row_part = lambda b: ps2[b % 2][:, :, 0:2 * (P + 1)].rearrange("p t (j d) -> p t j d", j=2)[:, :, :, P]
        column_part = lambda b: ps2[b % 2][:, 1, W - GB:W]
        w_loaded = sem("l0_w_loaded")
        x_loaded = [sem(f"x_loaded{b}") for b in range(RING)]
        adj_loaded = [sem(f"adj_loaded{b}") for b in range(RING)]
        kept = [sem(f"kept{b}") for b in range(RING)]
        (stats_done, moments_done, var_ready, rstd_ready, centred, rows_ready, pattern_done, rows_turned,
         adj_turned, hT_done, aT_done, first_done, columns_ready, u_done, own_done, columns_done, sums_done,
         ones_set, biased, row_done, rinv_done, second_done, gathered, x_done) = (
            sem("l0_" + n) for n in (
                "stats_done moments_done var_ready rstd_ready centred rows_ready pattern_done rows_turned "
                "adj_turned hT_done aT_done first_done columns_ready u_done own_done columns_done "
                "sums_done ones_set biased row_done rinv_done second_done gathered x_done").split())
        block = ctx.enter_context(nc.Block())

        def at_most_all(count):
            return min(count, NG) if isinstance(count, int) else count

        @block.sync
        def _(sp):
            sp.dma_start(wcat[:], c["l0_w_in"].rearrange("(t k) o -> k t o", t=2)).then_inc(w_loaded, 16)
            sp.dma_start(bias[:], c["l0_b_in"].rearrange("p (b d) -> p b d", b=GB)).then_inc(w_loaded, 16)

            def load(q, b):
                g = RING * q + b
                after(sp, stats_done, g - 3)
                nc.sync.nop(nofuse=True)
                sp.dma_start(graphs(cols(x, g)), c["x_in"][bass.ts(g, GB)].rearrange("b n d -> n b d"))\
                  .then_inc(x_loaded[b], 16)
                after(sp, columns_ready, g - 3)
                after(sp, pattern_done, g - 3)
                nc.sync.nop(nofuse=True)
                sp.dma_start(adj[b][:], c["adj_in"][bass.ts(g, GB)].rearrange("b n d -> n b d"))\
                  .then_inc(adj_loaded[b], 16)

            def keep(q, b):
                g = RING * q + b
                sp.wait_ge(aT_done, g + 1)
                nc.sync.nop(nofuse=True)
                sp.dma_start(graphs(cols(adjT, g)), aT[b % 2][:]).then_inc(kept[b], 16)

            staggered(sp, [(5, keep), (0, load)])
            for b in range(RING):
                sp.wait_ge(kept[b], 16 * NG // RING)

        @block.gpsimd
        def _(pool):
            def centre(q, b):
                g = RING * q + b
                pool.wait_ge(var_ready, g + 1)
                nc.gpsimd.tensor_tensor(rstd[b][:], var[b % 2][:], c["minus_half"][:], ALU.pow)\
                  .then_inc(rstd_ready, 1)
                after(pool, rows_turned, g - 3)
                nc.gpsimd.tensor_tensor(hn[b][:], graphs(cols(x, g)), per_node(mv[b % 2][:, :, 0:1]),
                                        ALU.subtract).then_inc(centred, 1)

            def add_bias(q, b):
                g = RING * q + b
                pool.wait_ge(own_done, g + 1)
                nc.gpsimd.tensor_tensor(pre[b % 2][:], pre[b % 2][:], bias[:], ALU.add).then_inc(biased, 1)

            staggered(pool, [(6, add_bias), (1, centre)])

        @block.vector
        def _(dve):
            def of(q, b):
                g = RING * q + b
                return statistics(nc, dve, lambda j: cols(x, g, j), stats[b % 2], stats_done, mv[b % 2],
                                  moments_done, var[b % 2][:], var_ready, g + 1)

            def raw(q, b):
                g = RING * q + b
                dve.wait_ge(x_loaded[b], dma_count(q, b, 0)[1])
                after(dve, centred, g - 1)
                of(q, b)[0]()

            def binary(q, b):
                g = RING * q + b
                dve.wait_ge(adj_loaded[b], dma_count(q, b, 0)[1])
                nc.vector.tensor_scalar(graphs(cols(pattern, g)), adj[b][:], 0.0, None, ALU.not_equal)\
                  .then_inc(pattern_done, 1)

            def column_sums(q, b):
                g = RING * q + b
                dve.wait_ge(columns_ready, g + 1)
                nc.vector.tensor_copy(sums[:, bass.ds(g * 2 * GB + GB, GB)], column_part(b))\
                  .then_inc(columns_done, 1)

            def row_sums(q, b):
                g = RING * q + b
                dve.wait_ge(second_done, g + 1)
                dve.wait_ge(columns_ready, at_most_all(g + 3))
                nc.vector.tensor_copy(sums[:, bass.ds(g * 2 * GB, GB)].rearrange("p (t j) -> p t j", t=2),
                                      row_part(b)).then_inc(sums_done, 1)

            def safe_sums(q, b):
                g = RING * q + b
                dve.wait_ge(sums_done, g + 1)
                nc.vector.tensor_scalar(rinv[b % 2][:], sums[:, bass.ds(g * 2 * GB, GB)], ROW_EPS, None, ALU.add)\
                  .then_inc(row_done, 1)

            def inverse(q, b):
                dve.wait_ge(row_done, RING * q + b + 1)
                nc.vector.reciprocal(rinv[b % 2][:], rinv[b % 2][:]).then_inc(rinv_done, 1)

            def gather(q, b):
                g = RING * q + b
                dve.wait_ge(biased, g + 1)
                dve.wait_ge(rinv_done, g + 1)
                for j in range(GB):
                    last = nc.vector.scalar_tensor_tensor(pre[b % 2][:, j, :], of_graph(b, j)[:, 0:P],
                                                          rinv[b % 2][:, j:j + 1], pre[b % 2][:, j, :],
                                                          ALU.mult, ALU.add)
                last.then_inc(gathered, 1)

            def close(q, b):
                g = RING * q + b
                dve.wait_ge(gathered, g + 1)
                nc.vector.scalar_tensor_tensor(cols(x, g), pre[b % 2][:].rearrange("p b d -> p (b d)"), 0.0,
                                               cols(x, g), ALU.max, ALU.add).then_inc(x_done, 1)

            for b in range(2):
                nc.vector.memset(u[b][:, :, P:P + 1], 1.0).then_inc(ones_set, 1)
            staggered(dve, [(1, raw), (6, row_sums), (1, lambda q, b: of(q, b)[1]()), (6, safe_sums),
                            (4, column_sums), (1, lambda q, b: of(q, b)[2]()), (6, inverse), (3, binary),
                            (6, gather), (6, close)])
            dve.wait_ge(x_done, NG)

        @block.scalar
        def _(act):
            def scale(q, b):
                g = RING * q + b
                act.wait_ge(centred, g + 1)
                act.wait_ge(rstd_ready, g + 1)
                for j in range(GB):
                    last = nc.scalar.activation(hn[b][:, j, :], hn[b][:, j, :], ACT.Copy,
                                                scale=rstd[b][:, j:j + 1])
                last.then_inc(rows_ready, 1)

            def turned(q, b):
                g = RING * q + b
                act.wait_ge(rows_turned, g + 1)
                after(act, first_done, g - 1)
                nc.scalar.activation(hT[b % 2][:], psH[:], ACT.Relu).then_inc(hT_done, 1)
                act.wait_ge(adj_turned, g + 1)
                after(act, second_done, g - 1)
                before, count = dma_count(q, b, 2)
                after(act, kept[before], count)
                nc.scalar.activation(aT[b % 2][:], psA[:], ACT.Copy).then_inc(aT_done, 1)

            def products(q, b):
                g = RING * q + b
                act.wait_ge(first_done, g + 1)
                after(act, second_done, g - 1)
                nc.scalar.activation(u[b % 2][:, :, 0:P], ps1[:, :, P:2 * P], ACT.Copy).then_inc(u_done, 1)
                after(act, x_done, g - 1)
                nc.scalar.activation(pre[b % 2][:], ps1[:, :, 0:P], ACT.Copy).then_inc(own_done, 1)

            staggered(act, [(4, turned), (5, products), (2, scale)])
            act.wait_ge(own_done, NG)

        @block.tensor
        def _(pe):
            def turn(q, b):
                g = RING * q + b
                pe.wait_ge(adj_loaded[b], dma_count(q, b, 0)[1])
                after(pe, aT_done, g)
                for j in range(GB):
                    last = nc.tensor.transpose(psA[:, j, :], adj[b][:, j, :], c["ident"][:])
                last.then_inc(adj_turned, 1)
                pe.wait_ge(rows_ready, g + 1)
                after(pe, hT_done, g)
                for j in range(GB):
                    last = nc.tensor.transpose(psH[:, j, :], hn[b][:, j, :], c["ident"][:])
                last.then_inc(rows_turned, 1)

            def columns(q, b):
                g = RING * q + b
                after(pe, columns_done, g - 1)
                for j in range(GB):
                    last = nc.tensor.matmul(column_part(b)[:, j:j + 1], adj[b][:, j, :], c["ones"][:],
                                            start=True, stop=True)
                last.then_inc(columns_ready, 1)

            def first(q, b):
                g = RING * q + b
                pe.wait_ge(hT_done, g + 1)
                after(pe, own_done, g)
                for j in range(GB):
                    last = nc.tensor.matmul(ps1[:, j, :], hT[b % 2][:, j, :],
                                            wcat[:].rearrange("k t o -> k (t o)"), start=True, stop=True)
                last.then_inc(first_done, 1)

            def second(q, b):
                g = RING * q + b
                pe.wait_ge(u_done, g + 1)
                after(pe, gathered, g - 1)
                pe.wait_ge(columns_done, g + 1)
                for j in range(GB):
                    last = nc.tensor.matmul(of_graph(b, j), aT[b % 2][:, j, :], u[b % 2][:, j, :],
                                            start=True, stop=True)
                last.then_inc(second_done, 1)

            pe.wait_ge(w_loaded, 32)
            pe.wait_ge(ones_set, 2)
            staggered(pe, [(4, turn), (6, second), (4, columns), (5, first)])


def layer1(nc, c):
    x, pattern, w_hi, w_lo, sums, no_sum = (c[n] for n in "x pattern w_hi w_lo sums no_sum".split())
    R_, Z_, N_ = range(GATES)
    with ExitStack() as ctx:
        sb = lambda name, shape, dt=F32: ctx.enter_context(nc.sbuf_tensor(name, shape, dt))
        sem = lambda name: ctx.enter_context(nc.semaphore(name))
        ps = lambda name: ctx.enter_context(nc.psum_tensor(name, [P, W], F32))
        state = [sb(f"state{j}", [P, W]) for j in range(SLOTS)]
        state_hi = [sb(f"state_hi{j}", [P, W], F16) for j in range(SLOTS)]
        state_lo = [sb(f"state_lo{j}", [P, W], F16) for j in range(SLOTS)]
        node_hi = [sb(f"node_hi{b}", [P, W], F16) for b in range(2)]
        node_lo = [sb(f"node_lo{b}", [P, W], F16) for b in range(2)]
        agg_hi = [sb(f"agg_hi{b}", [P, W], F16) for b in range(2)]
        agg_lo = [sb(f"agg_lo{b}", [P, W], F16) for b in range(2)]
        cand = [sb(f"cand{b}", [P, W]) for b in range(2)]
        zgate = [sb(f"zgate{b}", [P, W]) for b in range(2)]
        diff = sb("diff", [P, W])
        rows = sb("rows", [P, W])
        stats = sb("l1_stats", [P, GB, 6])
        mv = sb("l1_mv", [P, GB, 2])
        var = sb("l1_var", [P, GB])
        rstd = sb("l1_rstd", [P, GB])
        psT = [ps(f"psT{b}") for b in range(2)]
        psQ = [ps(f"psQ{b}") for b in range(2)]
        psR, psZ, psI, psH = ps("psR"), ps("psZ"), ps("psI"), ps("psHn")
        (r_ready, z_ready, i_ready, h_ready, r_done, z_done, reset_done, pre_done, n_done, diff_done,
         gated, state_new) = (sem(n) for n in (
             "r_ready z_ready i_ready h_ready r_done z_done reset_done pre_done n_done diff_done "
             "gated state_new").split())
        (turned, node_hi_done, node_ready, agg_ready, agg_hi_done, agg_split, state_hi_done,
         state_ready) = (sem(n) for n in (
             "turned node_hi_done node_ready agg_ready agg_hi_done agg_split state_hi_done state_ready").split())
        (stats_done, moments_done, var_ready, rstd_ready, centred, rows_ready, out_turned, out_done) = (
            sem("l1_" + n) for n in (
                "stats_done moments_done var_ready rstd_ready centred rows_ready out_turned out_done").split())
        no_sum_done, sums_safe, roots_done = sem("no_sum_done"), sem("sums_safe"), sem("roots_done")
        block = ctx.enter_context(nc.Block())


        def place(q, k):
            slot = k % SLOTS
            since = k - STAGGER * slot
            group = SLOTS * (q + since // QUAD) + slot
            busy = not isinstance(group, int) or 0 <= group < NG
            return busy, since % QUAD < SLOTS, group, since % QUAD // SLOTS

        def steps_before(q, k):
            if isinstance(q, int):
                return sum(place(0, p)[0] for p in range(QUAD * q + k))
            return q * QUAD + (k - EMPTY)

        def quads(eng, step):
            for k in range(QUAD):
                step(0, k)
            with eng.Fori(1, NQ - 1) as q:
                for k in range(QUAD):
                    step(q, k)
            for k in range(QUAD + STAGGER * (SLOTS - 1) - 1):
                step(NQ - 1, k)

        def enters(q, k, by):
            busy, new, group, _ = place(q, k + by)
            return busy and new, group

        @block.tensor
        def _(pe):
            def gate(bank, gate_at, layer, hi, lo, start, stop):
                w_at = bass.ts(gate_at, P)
                nc.tensor.matmul(bank[:], w_hi[:, layer, w_at], hi, start=start, stop=False)
                nc.tensor.matmul(bank[:], w_hi[:, layer, w_at], lo, start=False, stop=False)
                return nc.tensor.matmul(bank[:], w_lo[:, layer, w_at], hi, start=False, stop=stop)

            def turn(bank, src):
                for j in range(GB):
                    last = nc.tensor.transpose(bank[:, bass.ts(j, P)], src[:, bass.ts(j, P)], c["ident"][:])
                return last

            def transposes(q, k):
                busy, new, group, _ = place(q, k)
                b = k % 2
                if new:
                    left = group - SLOTS
                    if not (isinstance(left, int) and left < 0):
                        pe.wait_ge(state_new, steps_before(q, k - SLOTS + 1))
                        pe.wait_ge(node_ready, steps_before(q, k - 1))
                        after(pe, out_done, left - 1)
                        turn(psT[b], state[k % SLOTS]).then_inc(out_turned, 1)
                    if busy:
                        pe.wait_ge(rows_ready, group + 1)
                        after(pe, node_ready, steps_before(q, k))
                        turn(psT[1 - b], rows).then_inc(turned, 1)
                elif busy:
                    pe.wait_ge(state_new, steps_before(q, k - SLOTS + 1))
                    after(pe, node_ready, steps_before(q, k - 1))
                    past = k % STAGGER
                    started = place(q, k - past)[2]
                    if past == 1 or isinstance(q, int):
                        pe.wait_ge(state_hi_done, steps_before(q, k - past + 1))
                    if past == 2 or isinstance(q, int):
                        after(pe, out_done, started - SLOTS + 1)
                    turn(psT[b], state[k % SLOTS]).then_inc(turned, 1)

            def aggregate(q, k):
                busy, _, group, _ = place(q, k)
                if not busy:
                    return
                b = k % 2
                pe.wait_ge(node_ready, steps_before(q, k + 1))
                after(pe, agg_split, steps_before(q, k - 1))
                for j in range(GB):
                    at = bass.ts(j, P)
                    nc.tensor.matmul(psQ[b][:, at], node_hi[b][:, at], cols(pattern, group, j),
                                     start=True, stop=False)
                    last = nc.tensor.matmul(psQ[b][:, at], node_lo[b][:, at], cols(pattern, group, j),
                                            start=False, stop=True)
                last.then_inc(agg_ready, 1)

            def step(q, k):
                busy, _, _, layer = place(q, k)
                slot, b = k % SLOTS, k % 2
                before, this = steps_before(q, k), steps_before(q, k + 1)
                hi, lo = state_hi[slot][:], state_lo[slot][:]
                if busy:
                    pe.wait_ge(state_ready, this)
                    after(pe, r_done, before)
                    gate(psR, R_, LAYERS, hi, lo, True, False)
                    after(pe, reset_done, before)
                    gate(psH, N_, LAYERS, hi, lo, True, True).then_inc(h_ready, 1)
                    after(pe, z_done, before)
                    gate(psZ, Z_, LAYERS, hi, lo, True, False)
                transposes(q, k + 2)
                if busy:
                    pe.wait_ge(agg_split, this)
                    gate(psR, R_, layer, agg_hi[b][:], agg_lo[b][:], False, True).then_inc(r_ready, 1)
                    after(pe, pre_done, before)
                    gate(psI, N_, layer, agg_hi[b][:], agg_lo[b][:], True, True).then_inc(i_ready, 1)
                aggregate(q, k + 1)
                if busy:
                    gate(psZ, Z_, layer, agg_hi[b][:], agg_lo[b][:], False, True).then_inc(z_ready, 1)

            transposes(0, 0)
            aggregate(0, 0)
            quads(pe, step)

        @block.scalar
        def _(act):
            def node_high(q, k):
                busy, new, group, _ = place(q, k)
                if not busy:
                    return
                b = k % 2
                if new:
                    act.wait_ge(rows_ready, group + 1)
                else:
                    act.wait_ge(turned, steps_before(q, k + 1))
                after(act, agg_ready, steps_before(q, k - 1))
                nc.scalar.activation(node_hi[b][:], rows[:] if new else psT[b][:], ACT.Copy, scale=SH)\
                  .then_inc(node_hi_done, 1)

            def first_state(q, k):
                if enters(q, k, 0)[0]:
                    slot, b = k % SLOTS, k % 2
                    act.wait_ge(turned, steps_before(q, k + 1))
                    nc.scalar.activation(state[slot][:], psT[1 - b][:], ACT.Copy)
                    nc.scalar.activation(state_hi[slot][:], psT[1 - b][:], ACT.Copy, scale=SH)\
                      .then_inc(state_hi_done, 1)

            def aggregate_hi(q, k):
                if place(q, k)[0]:
                    b = k % 2
                    act.wait_ge(agg_ready, steps_before(q, k + 1))
                    after(act, z_ready, steps_before(q, k - 1))
                    nc.scalar.activation(agg_hi[b][:], psQ[b][:], ACT.Copy).then_inc(agg_hi_done, 1)

            def step(q, k):
                busy = place(q, k)[0]
                b = k % 2
                before, this = steps_before(q, k), steps_before(q, k + 1)
                node_high(q, k + 2)
                if busy:
                    act.wait_ge(r_ready, this)
                    after(act, state_new, steps_before(q, k - 1))
                    nc.scalar.activation(cand[b][:], psR[:], ACT.Sigmoid, bias=c["brz"][:, 0:1],
                                         scale=c["gscale"][:]).then_inc(r_done, 1)
                aggregate_hi(q, k + 1)
                if busy:
                    act.wait_ge(z_ready, this)
                    after(act, gated, steps_before(q, k - 1))
                    nc.scalar.activation(zgate[b][:], psZ[:], ACT.Sigmoid, bias=c["brz"][:, 1:2],
                                         scale=c["gscale"][:]).then_inc(z_done, 1)
                first_state(q, k + 2)
                busy3, new3, _, _ = place(q, k + 3)
                if busy3 and not new3:
                    act.wait_ge(state_new, before)
                    slot = (k - 1) % SLOTS
                    nc.scalar.activation(state_hi[slot][:], state[slot][:], ACT.Copy, scale=SH)\
                      .then_inc(state_hi_done, 1)
                if busy:
                    act.wait_ge(pre_done, this)
                    nc.scalar.activation(cand[b][:], cand[b][:], ACT.Tanh, bias=c["bin"][:],
                                         scale=c["gscale"][:]).then_inc(n_done, 1)

            nc.scalar.preload_act_table_set("sigmoid_and_others")
            node_high(0, 0)
            first_state(0, 0)
            aggregate_hi(0, 0)
            quads(act, step)

        @block.gpsimd
        def _(pool):
            def root(group):
                pool.wait_ge(var_ready, group + 1)
                after(pool, rows_ready, group)
                nc.gpsimd.tensor_tensor(rstd[:], var[:], c["minus_half"][:], ALU.pow).then_inc(rstd_ready, 1)

            def centre(q, k, group):
                last_start = steps_before(q, k - STAGGER + 1)
                after(pool, turned, last_start)
                after(pool, node_ready, last_start)
                nc.gpsimd.tensor_tensor(graphs(rows[:]), graphs(cols(x, group)), per_node(mv[:, :, 0:1]),
                                        ALU.subtract).then_inc(centred, 1)

            def root_of_sums(q, part):
                at = sums[:, bass.ds(q * 2 * GB * SLOTS + part * GB, GB)]
                nc.gpsimd.tensor_tensor(at, at, c["minus_half"][:], ALU.pow).then_inc(roots_done, 1)

            def step(q, k):
                busy = place(q, k)[0]
                slot, b = k % SLOTS, k % 2
                before, this = steps_before(q, k), steps_before(q, k + 1)
                if busy:
                    pool.wait_ge(n_done, this)
                    after(pool, state_new, before)
                    nc.gpsimd.tensor_tensor(diff[:], state[slot][:], cand[b][:], ALU.subtract)\
                      .then_inc(diff_done, 1)
                    pool.wait_ge(diff_done, this)
                    pool.wait_ge(z_done, this)
                    nc.gpsimd.tensor_tensor(diff[:], diff[:], zgate[b][:], ALU.mult).then_inc(gated, 1)
                if enters(q, k, ROOT_AHEAD)[0]:
                    root(enters(q, k, ROOT_AHEAD)[1])
                if enters(q, k, CENTRE_AHEAD)[0]:
                    centre(q, k + CENTRE_AHEAD, enters(q, k, CENTRE_AHEAD)[1])
                if k % STAGGER in (1, 2) and k < QUAD:
                    root_of_sums(q, 2 * (k // STAGGER) + k % STAGGER - 1)

            for j in range(2):
                root(j)
                centre(0, STAGGER * j, j)
            pool.wait_ge(sums_safe, 1)
            quads(pool, step)
            pool.wait_ge(roots_done, NQ * 2 * SLOTS)

        @block.vector
        def _(dve):
            def of(group):
                return statistics(nc, dve, lambda j: cols(x, group, j), stats, stats_done, mv,
                                  moments_done, var[:], var_ready, group + 1)

            def raw(group):
                after(dve, moments_done, group)
                of(group)[0]()

            def moments(group):
                after(dve, centred, group)
                raw_, moments_, variance_ = of(group)
                moments_()
                after(dve, rstd_ready, group)
                variance_()

            def make_rows(group):
                dve.wait_ge(centred, group + 1)
                dve.wait_ge(rstd_ready, group + 1)
                for j in range(GB):
                    last = nc.vector.tensor_scalar(rows[:, bass.ts(j, P)], rows[:, bass.ts(j, P)],
                                                   rstd[:, j:j + 1], 0.0, ALU.mult, ALU.max)
                last.then_inc(rows_ready, 1)

            def node_low(q, k):
                busy, new, _, _ = place(q, k)
                if busy:
                    b = k % 2
                    dve.wait_ge(node_hi_done, steps_before(q, k + 1))
                    nc.vector.scalar_tensor_tensor(node_lo[b][:], rows[:] if new else psT[b][:], SH, node_hi[b][:],
                                                   ALU.mult, ALU.subtract).then_inc(node_ready, 1)

            def state_low(q, k):
                slot = k % SLOTS
                dve.wait_ge(state_hi_done, steps_before(q, k + 1))
                nc.vector.scalar_tensor_tensor(state_lo[slot][:], state[slot][:], SH, state_hi[slot][:],
                                               ALU.mult, ALU.subtract).then_inc(state_ready, 1)

            def aggregate_low(q, k):
                if place(q, k)[0]:
                    b = k % 2
                    dve.wait_ge(agg_hi_done, steps_before(q, k + 1))
                    nc.vector.tensor_tensor(agg_lo[b][:], psQ[b][:], agg_hi[b][:], ALU.subtract)\
                       .then_inc(agg_split, 1)

            def leave(group, b):
                dve.wait_ge(out_turned, group + 1)
                for j in range(GB):
                    last = nc.vector.scalar_tensor_tensor(
                        cols(x, group, j), psT[b][:, bass.ts(j, P)],
                        c["mask"][:, bass.ds(group * GB + j, 1)], cols(x, group, j), ALU.mult, ALU.add)
                last.then_inc(out_done, 1)

            def update(q, k):
                if place(q, k)[0]:
                    dve.wait_ge(gated, steps_before(q, k + 1))
                    nc.vector.tensor_tensor(state[k % SLOTS][:], cand[k % 2][:], diff[:], ALU.add)\
                      .then_inc(state_new, 1)

            def step(q, k):
                busy = place(q, k)[0]
                b = k % 2
                this = steps_before(q, k + 1)
                node_low(q, k + 2)
                if busy:
                    dve.wait_ge(r_done, this)
                    dve.wait_ge(h_ready, this)
                    nc.vector.scalar_tensor_tensor(cand[b][:], psH[:], c["bhn"][:], cand[b][:], ALU.add, ALU.mult)\
                      .then_inc(reset_done, 1)
                aggregate_low(q, k + 1)
                update(q, k - 1)
                if busy:
                    dve.wait_ge(reset_done, this)
                    dve.wait_ge(i_ready, this)
                    nc.vector.tensor_tensor(cand[b][:], cand[b][:], psI[:], ALU.add).then_inc(pre_done, 1)
                _, new2, group2, _ = place(q, k + 2)
                if enters(q, k, 2)[0]:
                    state_low(q, k + 2)
                busy3, new3, _, _ = place(q, k + 3)
                if busy3 and not new3:
                    state_low(q, k + 3)
                if new2 and not (isinstance(group2, int) and group2 < SLOTS):
                    leave(group2 - SLOTS, b)
                for by, prepare_group in ((RAW_AHEAD, raw), (MOMENTS_AHEAD, moments), (ROWS_AHEAD, make_rows)):
                    if enters(q, k, by)[0]:
                        prepare_group(enters(q, k, by)[1])

            nc.vector.tensor_scalar(no_sum[:], sums[:], 0.0, None, ALU.is_equal).then_inc(no_sum_done, 1)
            raw(0)
            moments(0)
            dve.wait_ge(no_sum_done, 1)
            nc.vector.tensor_tensor(sums[:], sums[:], no_sum[:], ALU.add).then_inc(sums_safe, 1)
            make_rows(0)
            raw(1)
            moments(1)
            node_low(0, 0)
            state_low(0, 0)
            aggregate_low(0, 0)
            quads(dve, step)
            dve.wait_ge(out_done, NG)


def layer2(nc, c):
    x, adjT, sums = c["x"], c["adjT"], c["sums"]
    with ExitStack() as ctx:
        sb = lambda name, shape, dt=F32: ctx.enter_context(nc.sbuf_tensor(name, shape, dt))
        sem = lambda name: ctx.enter_context(nc.semaphore(name))
        ring = lambda name, n, shape, dt=F32: [sb(f"l2_{name}{b}", shape, dt) for b in range(n)]
        ps = lambda name, shape: ctx.enter_context(nc.psum_tensor(name, shape, F32))
        wcat = sb("l2_wcat", [P, 2, P])
        gb = sb("l2_gb", [P, 2])
        has_sum = sb("l2_has_sum", [P, NG * 2 * GB])
        rows = ring("rows", RING, [P, GB, P])
        xn = ring("xn", RING, [P, GB, P])
        aS = ring("aS", 2, [P, GB, P])
        xnT = ring("xnT", 2, [P, GB, P])
        u = ring("u", 2, [P, GB, P])
        own = ring("own", RING, [P, GB, P])
        pre = ring("pre", RING, [P, GB, P])
        soft = ring("soft", RING, [P, GB, P])
        stats = ring("stats", 2, [P, GB, 6])
        mv = ring("mv", 2, [P, GB, 2])
        inner = ring("inner", 2, [P, GB])
        stats2 = ring("stats2", 2, [P, GB, 6])
        mv2 = ring("mv2", RING, [P, GB, 2])
        var2 = ring("var2", 2, [P, GB])
        rstd2 = ring("rstd2", RING, [P, GB])
        psX = [ps(f"l2_psX{b}", [P, GB, P]) for b in range(2)]
        ps1 = [ps(f"l2_ps1{b}", [P, GB, 2 * P]) for b in range(2)]
        ps2 = [ps(f"l2_ps2{b}", [P, GB, P]) for b in range(2)]
        (w_loaded, w_link, w_ready, stats_done, moments_done, inner_ready, rows_ready,
         stats2_done, moments2_done, var2_ready, rstd2_ready, centred, xn_ready, aS_ready, xn_turned, xnT_done,
         first_done, u_done, own_done, second_done, pre_done, abs_done, exp_done, log_done, soft_done,
         x_done) = (
            sem("l2_" + n) for n in (
                "w_loaded w_link w_ready stats_done moments_done inner_ready rows_ready "
                "stats2_done moments2_done var2_ready rstd2_ready centred xn_ready aS_ready xn_turned xnT_done "
                "first_done u_done own_done second_done pre_done abs_done exp_done log_done soft_done "
                "x_done").split())
        block = ctx.enter_context(nc.Block())

        @block.sync
        def _(sp):
            sp.dma_start(wcat[:, 0, :], c["l2_ws_in"]).then_inc(w_loaded, 16)
            sp.dma_start(wcat[:, 1, :], c["l2_wn_in"]).then_inc(w_loaded, 16)
            sp.dma_start(gb[:], c["l2_gb_in"]).then_inc(w_loaded, 16)

        @block.gpsimd
        def _(pool):
            def root2(q, b):
                g = RING * q + b
                pool.wait_ge(var2_ready, g + 1)
                nc.gpsimd.tensor_tensor(rstd2[b][:], var2[b % 2][:], c["minus_half"][:], ALU.pow)\
                  .then_inc(rstd2_ready, 1)

            def centre(q, b):
                g = RING * q + b
                pool.wait_ge(moments2_done, g + 1)
                after(pool, xn_turned, g - 3)
                nc.gpsimd.tensor_tensor(xn[b][:], rows[b][:], per_node(mv2[b][:, :, 0:1]), ALU.subtract)\
                  .then_inc(centred, 1)

            def scale_adj(q, b):
                g = RING * q + b
                after(pool, second_done, g - 1)
                s_in = sums[:, bass.ds(g * 2 * GB, GB)].rearrange("p (j o) -> p j o", o=1)
                nc.gpsimd.tensor_tensor(aS[b % 2][:], graphs(cols(adjT, g)), per_node(s_in), ALU.mult)\
                  .then_inc(aS_ready, 1)

            def add(q, b):
                g = RING * q + b
                pool.wait_ge(soft_done, g + 1)
                nc.gpsimd.tensor_tensor(graphs(cols(x, g)), graphs(cols(x, g)), soft[b][:], ALU.add)\
                  .then_inc(x_done, 1)

            pool.wait_ge(w_ready, 1)
            staggered(pool, [(10, add), (2, centre), (2, root2), (5, scale_adj)])
            pool.wait_ge(x_done, NG)

        @block.vector
        def _(dve):
            def raw(q, b):
                g = RING * q + b
                after(dve, moments_done, g - 1)
                for j in range(GB):
                    last = nc.vector.bn_stats(stats[b % 2][:, j, :], cols(x, g, j))
                last.then_inc(stats_done, 1)

            def moments(q, b):
                g = RING * q + b
                after(dve, rows_ready, g - 1)
                after(dve, inner_ready, g - 1)
                dve.wait_ge(stats_done, g + 1)
                nc.vector.nop(nofuse=True)
                for j in range(GB):
                    last = nc.vector.bn_aggr(mv[b % 2][:, j, :], stats[b % 2][:, j, :])
                last.then_inc(moments_done, 1)

            def clip(q, b):
                g = RING * q + b
                dve.wait_ge(moments_done, g + 1)
                after(dve, centred, g - 3)
                for j in range(GB):
                    last = nc.vector.tensor_scalar(rows[b][:, j, :], cols(x, g, j), mv[b % 2][:, j, 0:1], 0.0,
                                                   ALU.subtract, ALU.max)
                last.then_inc(rows_ready, 1)
                after(dve, var2_ready, g - 1)
                nc.vector.tensor_scalar(inner[b % 2][:], mv[b % 2][:, :, 1], LN_EPS, LN_EPS ** 2,
                                        ALU.mult, ALU.add).then_inc(inner_ready, 1)

            def raw2(q, b):
                g = RING * q + b
                dve.wait_ge(rows_ready, g + 1)
                for j in range(GB):
                    last = nc.vector.bn_stats(stats2[b % 2][:, j, :], rows[b][:, j, :])
                last.then_inc(stats2_done, 1)

            def moments2(q, b):
                g = RING * q + b
                dve.wait_ge(stats2_done, g + 1)
                nc.vector.nop(nofuse=True)
                for j in range(GB):
                    last = nc.vector.bn_aggr(mv2[b][:, j, :], stats2[b % 2][:, j, :])
                last.then_inc(moments2_done, 1)

            def variance2(q, b):
                g = RING * q + b
                dve.wait_ge(moments2_done, g + 1)
                dve.wait_ge(inner_ready, g + 1)
                after(dve, rstd2_ready, g - 1)
                nc.vector.tensor_tensor(var2[b % 2][:], mv2[b][:, :, 1], inner[b % 2][:], ALU.add)\
                  .then_inc(var2_ready, 1)

            def outer(q, b):
                g = RING * q + b
                dve.wait_ge(second_done, g + 1)
                dve.wait_ge(own_done, g + 1)
                for j in range(GB):
                    last = nc.vector.scalar_tensor_tensor(pre[b][:, j, :], ps2[b % 2][:, j, :],
                                                          sums[:, bass.ds(g * 2 * GB + GB + j, 1)],
                                                          own[b][:, j, :], ALU.mult, ALU.add)
                last.then_inc(pre_done, 1)

            def finish(q, b):
                g = RING * q + b
                dve.wait_ge(log_done, g + 1)
                flat = lambda tile: tile[:].rearrange("p b d -> p (b d)")
                nc.vector.scalar_tensor_tensor(flat(soft[b]), flat(pre[b]), 0.0, flat(soft[b]),
                                               ALU.max, ALU.add).then_inc(soft_done, 1)

            dve.wait_ge(w_loaded, 48)
            nc.vector.tensor_tensor(wcat[:, 0, :], wcat[:, 0, :], wcat[:, 1, :], ALU.add)
            nc.vector.tensor_scalar(has_sum[:], c["no_sum"][:], -1.0, 1.0, ALU.mult, ALU.add).then_inc(w_link, 1)
            dve.wait_ge(w_link, 1)
            nc.vector.tensor_tensor(sums[:], sums[:], has_sum[:], ALU.mult).then_inc(w_link, 1)
            dve.wait_ge(w_link, 2)
            outer_part = sums[:].rearrange("p (g t j) -> p g t j", t=2, j=GB)[:, :, 1, :]
            nc.vector.tensor_scalar(outer_part, outer_part, -1.0, None, ALU.mult).then_inc(w_ready, 1)
            dve.wait_ge(w_ready, 1)
            staggered(dve, [(9, finish), (1, clip), (7, outer), (1, raw2), (0, raw), (1, moments2),
                            (0, moments), (1, variance2)])

        @block.scalar
        def _(act):
            def scale(q, b):
                g = RING * q + b
                act.wait_ge(centred, g + 1)
                act.wait_ge(rstd2_ready, g + 1)
                for j in range(GB):
                    last = nc.scalar.activation(xn[b][:, j, :], xn[b][:, j, :], ACT.Copy,
                                                scale=rstd2[b][:, j:j + 1])
                last.then_inc(xn_ready, 1)

            def turned(q, b):
                g = RING * q + b
                act.wait_ge(xn_turned, g + 1)
                after(act, first_done, g - 1)
                nc.scalar.activation(xnT[b % 2][:], psX[b % 2][:], ACT.Identity, bias=gb[:, 1:2],
                                     scale=gb[:, 0:1]).then_inc(xnT_done, 1)

            def products(q, b):
                g = RING * q + b
                act.wait_ge(first_done, g + 1)
                after(act, second_done, g - 1)
                nc.scalar.activation(u[b % 2][:], ps1[b % 2][:, :, P:2 * P], ACT.Copy).then_inc(u_done, 1)
                after(act, pre_done, g - 3)
                nc.scalar.activation(own[b][:], ps1[b % 2][:, :, 0:P], ACT.Copy).then_inc(own_done, 1)

            def magnitude(q, b):
                g = RING * q + b
                act.wait_ge(pre_done, g + 1)
                after(act, x_done, g - 3)
                nc.scalar.activation(soft[b][:], pre[b][:], ACT.Abs).then_inc(abs_done, 1)

            def exponential(q, b):
                act.wait_ge(abs_done, RING * q + b + 1)
                nc.scalar.activation(soft[b][:], soft[b][:], ACT.Exp, scale=-1.0).then_inc(exp_done, 1)

            def logarithm(q, b):
                act.wait_ge(exp_done, RING * q + b + 1)
                nc.scalar.activation(soft[b][:], soft[b][:], ACT.Ln, bias=1.0).then_inc(log_done, 1)

            nc.scalar.preload_act_table_set("natural_log_exp_and_others")
            act.wait_ge(w_loaded, 48)
            staggered(act, [(4, turned), (8, magnitude), (3, scale), (8, exponential), (5, products),
                            (8, logarithm)])

        @block.tensor
        def _(pe):
            def turn(q, b):
                g = RING * q + b
                pe.wait_ge(xn_ready, g + 1)
                after(pe, xnT_done, g - 1)
                for j in range(GB):
                    last = nc.tensor.transpose(psX[b % 2][:, j, :], xn[b][:, j, :], c["ident"][:])
                last.then_inc(xn_turned, 1)

            def first(q, b):
                g = RING * q + b
                pe.wait_ge(xnT_done, g + 1)
                after(pe, own_done, g - 1)
                for j in range(GB):
                    last = nc.tensor.matmul(ps1[b % 2][:, j, :], xnT[b % 2][:, j, :],
                                            wcat[:].rearrange("k t o -> k (t o)"), start=True, stop=True)
                last.then_inc(first_done, 1)

            def second(q, b):
                g = RING * q + b
                pe.wait_ge(u_done, g + 1)
                pe.wait_ge(aS_ready, g + 1)
                after(pe, pre_done, g - 1)
                for j in range(GB):
                    last = nc.tensor.matmul(ps2[b % 2][:, j, :], aS[b % 2][:, j, :], u[b % 2][:, j, :],
                                            start=True, stop=True)
                last.then_inc(second_done, 1)

            pe.wait_ge(w_ready, 1)
            staggered(pe, [(4, turn), (6, second), (5, first)])


def layer3(nc, c):
    x, adjT = c["x"], c["adjT"]
    HID = 2
    with ExitStack() as ctx:
        sb = lambda name, shape, dt=F32: ctx.enter_context(nc.sbuf_tensor(name, shape, dt))
        sem = lambda name: ctx.enter_context(nc.semaphore(name))
        ring = lambda name, n, shape, dt=F32: [sb(f"l3_{name}{b}", shape, dt) for b in range(n)]
        ps = lambda name, shape: ctx.enter_context(nc.psum_tensor(name, shape, F32))
        w1 = sb("l3_w1", [P, HID, P])
        w2 = sb("l3_w2", [P, HID, P])
        b1 = sb("l3_b1", [P, HID])
        b2 = sb("l3_b2", [P, GB, P])
        eps1 = sb("l3_eps1", [P, 1])
        self_loop = sb("l3_self_loop", [P, GB, P])
        rows = ring("rows", RING, [P, GB, P])
        aI = ring("aI", RING, [P, GB, P])
        gT = ring("gT", 2, [P, W])
        hid = ring("hid", 2, [P, HID, W])
        out = ring("out", RING, [P, GB, P])
        stats = ring("stats", 2, [P, GB, 6])
        mv = ring("mv", RING, [P, GB, 2])
        var = ring("var", 2, [P, GB])
        rstd = ring("rstd", RING, [P, GB])
        psG = [ps(f"l3_psG{b}", [P, W]) for b in range(2)]
        psA = [ps(f"l3_psA{b}", [P, HID, W]) for b in range(2)]
        psO = [ps(f"l3_psO{b}", [P, GB, P]) for b in range(2)]
        stored = [sem(f"l3_stored{b}") for b in range(RING)]
        (w_loaded, eps_ready, loop_ready, stats_done, moments_done, var_ready, rstd_ready, normed, rows_ready,
         aI_ready, mixed, gT_done, hidden, hid_done, projected, summed, out_ready) = (
            sem("l3_" + n) for n in (
                "w_loaded eps_ready loop_ready stats_done moments_done var_ready rstd_ready normed rows_ready "
                "aI_ready mixed gT_done hidden hid_done projected summed out_ready").split())
        block = ctx.enter_context(nc.Block())

        @block.sync
        def _(sp):
            for dst, src in ((w1[:], c["l3_w1_in"].rearrange("k (t o) -> k t o", t=HID)),
                             (w2[:], c["l3_w2_in"].rearrange("(t k) o -> k t o", t=HID)),
                             (b1[:], c["l3_b1_in"]), (b2[:], c["l3_b2_in"].rearrange("p (b d) -> p b d", b=GB)),
                             (eps1[:], c["l3_eps_in"])):
                sp.dma_start(dst, src).then_inc(w_loaded, 16)

            def store(q, b):
                g = RING * q + b
                sp.wait_ge(out_ready, g + 1)
                sp.dma_start(c["out"][bass.ts(g, GB)].rearrange("b n d -> n b d"), out[b][:])\
                  .then_inc(stored[b], 16)

            staggered(sp, [(0, store)])
            for b in range(RING):
                sp.wait_ge(stored[b], 16 * NG // RING)

        @block.gpsimd
        def _(pool):
            def root(q, b):
                g = RING * q + b
                pool.wait_ge(var_ready, g + 1)
                nc.gpsimd.tensor_tensor(rstd[b][:], var[b % 2][:], c["minus_half"][:], ALU.pow)\
                  .then_inc(rstd_ready, 1)

            def loops(q, b):
                g = RING * q + b
                after(pool, mixed, g - 3)
                nc.gpsimd.tensor_tensor(aI[b][:], graphs(cols(adjT, g)), self_loop[:], ALU.add)\
                  .then_inc(aI_ready, 1)

            def bias(q, b):
                g = RING * q + b
                pool.wait_ge(summed, g + 1)
                nc.gpsimd.tensor_tensor(out[b][:], out[b][:], b2[:], ALU.add).then_inc(out_ready, 1)

            pool.wait_ge(loop_ready, GB)
            staggered(pool, [(7, bias), (0, root), (1, loops)])

        @block.vector
        def _(dve):
            def of_x(q, b):
                g = RING * q + b
                return statistics(nc, dve, lambda j: cols(x, g, j), stats[b % 2], stats_done, mv[b],
                                  moments_done, var[b % 2][:], var_ready, g + 1)

            def raw(q, b):
                after(dve, rstd_ready, RING * q + b - 1)
                of_x(q, b)[0]()

            def norm(q, b):
                g = RING * q + b
                dve.wait_ge(rstd_ready, g + 1)
                after(dve, mixed, g - 3)
                for j in range(GB):
                    last = nc.vector.tensor_scalar(rows[b][:, j, :], cols(x, g, j), mv[b][:, j, 0:1],
                                                   rstd[b][:, j:j + 1], ALU.subtract, ALU.mult)
                last.then_inc(normed, 1)

            def clip(q, b):
                dve.wait_ge(normed, RING * q + b + 1)
                nc.vector.tensor_scalar(rows[b][:], rows[b][:], 0.0, None, ALU.max).then_inc(rows_ready, 1)

            def finish(q, b):
                g = RING * q + b
                dve.wait_ge(projected, g + 1)
                before, count = dma_count(q, b, RING)
                after(dve, stored[before], count)
                nc.vector.tensor_tensor(out[b][:], psO[b % 2][:], graphs(cols(x, g)), ALU.add)\
                  .then_inc(summed, 1)

            dve.wait_ge(w_loaded, 5 * 16)
            nc.vector.tensor_scalar(eps1[:], eps1[:], 1.0, None, ALU.add).then_inc(eps_ready, 1)
            dve.wait_ge(eps_ready, 1)
            for j in range(GB):
                nc.vector.tensor_scalar(self_loop[:, j, :], c["ident"][:], eps1[:], None, ALU.mult)\
                  .then_inc(loop_ready, 1)
            staggered(dve, [(0, raw), (1, norm), (0, lambda q, b: of_x(q, b)[1]()), (1, clip), (6, finish),
                            (0, lambda q, b: of_x(q, b)[2]())])

        @block.scalar
        def _(act):
            def mixed_rows(q, b):
                g = RING * q + b
                act.wait_ge(mixed, g + 1)
                after(act, hidden, g - 1)
                nc.scalar.activation(gT[b % 2][:], psG[b % 2][:], ACT.Copy).then_inc(gT_done, 1)

            def hidden_rows(q, b):
                g = RING * q + b
                act.wait_ge(hidden, g + 1)
                after(act, projected, g - 1)
                for t in range(HID):
                    last = nc.scalar.activation(hid[b % 2][:, t, :], psA[b % 2][:, t, :], ACT.Relu,
                                                bias=b1[:, t:t + 1])
                last.then_inc(hid_done, 1)

            act.wait_ge(w_loaded, 5 * 16)
            staggered(act, [(3, hidden_rows), (2, mixed_rows)])

        @block.tensor
        def _(pe):
            def mix(q, b):
                g = RING * q + b
                pe.wait_ge(rows_ready, g + 1)
                pe.wait_ge(aI_ready, g + 1)
                after(pe, gT_done, g - 1)
                for j in range(GB):
                    last = nc.tensor.matmul(psG[b % 2][:, bass.ts(j, P)], rows[b][:, j, :], aI[b][:, j, :],
                                            start=True, stop=True)
                last.then_inc(mixed, 1)

            def hide(q, b):
                g = RING * q + b
                pe.wait_ge(gT_done, g + 1)
                after(pe, hid_done, g - 1)
                for t in range(HID):
                    last = nc.tensor.matmul(psA[b % 2][:, t, :], w1[:, t, :], gT[b % 2][:], start=True, stop=True)
                last.then_inc(hidden, 1)

            def project(q, b):
                g = RING * q + b
                pe.wait_ge(hid_done, g + 1)
                after(pe, summed, g - 1)
                for j in range(GB):
                    for t in range(HID):
                        last = nc.tensor.matmul(psO[b % 2][:, j, :], hid[b % 2][:, t, bass.ts(j, P)], w2[:, t, :],
                                                start=(t == 0), stop=(t == HID - 1))
                last.then_inc(projected, 1)

            pe.wait_ge(w_loaded, 5 * 16)
            staggered(pe, [(5, project), (3, hide), (2, mix)])


def gnn_stack_kernel(nc, c):
    with ExitStack() as ctx:
        sb = lambda name, shape, dt=F32: ctx.enter_context(nc.sbuf_tensor(name, shape, dt))
        c["x"] = sb("x", [P, NG * W])
        c["adjT"] = sb("adjT", [P, NG * W])
        c["sums"] = sb("sums", [P, NG * 2 * GB])
        c["no_sum"] = sb("no_sum", [P, NG * 2 * GB], mybir.dt.uint8)
        c["w_hi"] = sb("w_hi", [P, LAYERS + 1, GATES * P], F16)
        c["w_lo"] = sb("w_lo", [P, LAYERS + 1, GATES * P], F16)
        c["ident"] = sb("ident", [P, P])
        c["ones"] = sb("ones", [P, 1])
        c["minus_half"] = sb("minus_half", [P, GB])
        c["mask"] = sb("mask", [P, GRAPHS])
        c["gscale"] = sb("gscale", [P, 1])
        c["bhn"] = sb("bhn", [P, 1])
        c["brz"] = sb("brz", [P, 2])
        c["bin"] = sb("bin", [P, 1])
        with nc.sbuf_tensor("pattern", [P, NG * W], F16) as c["pattern"]:
            prepare(nc, c)
            layer0(nc, c)
            layer1(nc, c)
        layer2(nc, c)
        layer3(nc, c)


def kernel(**inputs):
    import numpy as np
    import concourse.bacc as bacc
    from concourse.bass_utils import run_bass_kernel_spmd

    a = {k: np.asarray(v) for k, v in inputs.items()}
    column = lambda v, n: np.ascontiguousarray(v.reshape(n, P).T)
    spread = lambda v: np.ascontiguousarray(np.broadcast_to(np.tile(v, GB), (P, W)))
    arrays = {
        "x_in": a["x"], "adj_in": a["adj"],
        "mask_in": np.ascontiguousarray(a["nodemask"].T),
        "l0_w_in": a["L0_gnn_weight"], "l0_b_in": spread(a["L0_gnn_bias"]),
        "msgT_in": np.ascontiguousarray(a["L1_gnn_weight"].transpose(0, 2, 1)),
        "ihT_in": np.ascontiguousarray(a["L1_gnn_w_ih"].T), "hhT_in": np.ascontiguousarray(a["L1_gnn_w_hh"].T),
        "bih_in": column(a["L1_gnn_b_ih"], GATES), "bhh_in": column(a["L1_gnn_b_hh"], GATES),
        "l2_ws_in": a["L2_gnn_W_self"], "l2_wn_in": a["L2_gnn_W_neigh"],
        "l2_gb_in": np.ascontiguousarray(np.stack([a["L2_gnn_gamma"], a["L2_gnn_beta"]], axis=1)),
        "l3_w1_in": a["L3_gnn_W1"], "l3_b1_in": column(a["L3_gnn_b1"], 2),
        "l3_w2_in": a["L3_gnn_W2"], "l3_b2_in": spread(a["L3_gnn_b2"]),
        "l3_eps_in": np.ascontiguousarray(np.broadcast_to(a["L3_gnn_eps"], (P, 1))),
    }
    nc = bacc.Bacc("TRN2", target_bir_lowering=False, num_devices=1)
    c = {n: nc.dram_tensor(n, v.shape, mybir.dt.from_np(v.dtype), kind="ExternalInput").ap()
         for n, v in arrays.items()}
    c["out"] = nc.dram_tensor("out", (GRAPHS, P, P), F32, kind="ExternalOutput").ap()
    gnn_stack_kernel(nc, c)
    r = run_bass_kernel_spmd(nc, [arrays], core_ids=[0])
    return r.results[0]["out"]
```

```python
from contextlib import ExitStack

import concourse.bass as bass
from concourse import mybir
from concourse.alu_op_type import AluOpType as ALU

F32 = mybir.dt.float32
F16 = mybir.dt.float16
I32 = mybir.dt.int32
ACT = mybir.ActivationFunctionType
AX = mybir.AxisListType.X

P = 128
GRAPHS = 128
GB = 4
RING = 4
NG = GRAPHS // GB
W = GB * P
LAYERS = 5
GATES = 3
LN_EPS = 1e-5
ROW_EPS = 1e-8
SH = 32.0
SW = 256.0
SLOTS = 4
QUAD = LAYERS * SLOTS
STAGGER = 3
EMPTY = sum(STAGGER * j // SLOTS for j in range(SLOTS))
CENTRE_AHEAD, ROWS_AHEAD, STATS_FROM = 5, 4, 8
LEFT_STATS = (0, 3, 6, 17)
SCRATCH = 7
NQ = NG // SLOTS


def after(eng, sem, value):
    if not (isinstance(value, int) and value <= 0):
        eng.wait_ge(sem, value)


def staggered(eng, stages, then=(), shift=0):
    def plain(part, t):
        for lag, stage in part:
            if 0 <= t - lag < NG:
                stage((t - lag) // RING, (t - lag) % RING)

    def head_of(part):
        head = max(lag for lag, _ in part) + RING
        return head + -head % RING

    def looped(part):
        head = head_of(part)
        with eng.Fori(0, (NG - head) // RING) as i:
            for u in range(RING):
                for lag, stage in part:
                    k = head + u - lag
                    stage(i + k // RING, k % RING)

    for t in range(head_of(stages)):
        plain(stages, t)
    looped(stages)
    if then:
        for t in range(NG, NG + shift + head_of(then)):
            plain(stages, t)
            plain(then, t - NG - shift)
        looped(then)
        stages = then
    for t in range(NG, NG + head_of(stages) - RING):
        plain(stages, t)


def at_ticks(tasks):
    def stage(q, b):
        if isinstance(q, int) and RING * q + b in tasks:
            tasks[RING * q + b]()

    return 0, stage


def dma_count(q, b, back):
    return (b - back) % RING, 16 * (q + (b - back) // RING + 1)


def cols(tile, g, j=None):
    return tile[:, bass.ds(g * W, W)] if j is None else tile[:, bass.ds(g * W + j * P, P)]


def graphs(ap):
    return ap.rearrange("p (b d) -> p b d", b=GB)


def statistics(nc, dve, x_of, stats, stats_done, mv, moments_done, var, var_ready, nth):
    def raw():
        for j in range(GB):
            last = nc.vector.bn_stats(stats[:, j, :], x_of(j))
        last.then_inc(stats_done, 1)

    def moments():
        dve.wait_ge(stats_done, nth)
        nc.vector.nop(nofuse=True)
        for j in range(GB):
            last = nc.vector.bn_aggr(mv[:, j, :], stats[:, j, :])
        last.then_inc(moments_done, 1)

    def variance():
        dve.wait_ge(moments_done, nth)
        nc.vector.tensor_scalar(var, mv[:, :, 1], LN_EPS, None, ALU.add).then_inc(var_ready, 1)

    return raw, moments, variance


def per_node(ap):
    return ap.to_broadcast([P, GB, P])


def layer0(nc, c):
    x, adjT, pattern, sums = c["x"], c["adjT"], c["pattern"], c["sums"]
    with ExitStack() as ctx:
        sb = lambda name, shape, dt=F32: ctx.enter_context(nc.sbuf_tensor(name, shape, dt))
        sem = lambda name: ctx.enter_context(nc.semaphore(name))
        ring = lambda name, n, shape, dt=F32: [sb(f"l0_{name}{b}", shape, dt) for b in range(n)]
        ps = lambda name, shape: ctx.enter_context(nc.psum_tensor(name, shape, F32))
        wcat = sb("l0_wcat", [P, 2, P])
        bias = sb("l0_bias", [P, 1, P])
        adj = ring("adj", RING, [P, GB, P])
        hn = ring("hn", RING, [P, GB, P])
        hT = ring("hT", 2, [P, GB, P])
        aT = ring("aT", 2, [P, GB, P])
        u = ring("u", 2, [P, GB, P + 1])
        pre = ring("pre", 2, [P, GB, P])
        stats = ring("stats", 2, [P, GB, 6])
        mv = ring("mv", 2, [P, GB, 2])
        var = ring("var", 2, [P, GB])
        rstd = ring("rstd", RING, [P, GB])
        rinv = ring("rinv", 2, [P, GB])
        psA, psH = ps("l0_psA", [P, GB, P]), ps("l0_psH", [P, GB, P])
        ps1 = ps("l0_ps1", [P, GB, 2 * P])
        ps2 = [ps(f"l0_ps2{b}", [P, 2, W]) for b in range(2)]
        of_graph = lambda b, j: ps2[b % 2][:, j // 2, bass.ds(j % 2 * (P + 1), P + 1)]
        row_part = lambda b: ps2[b % 2][:, :, 0:2 * (P + 1)].rearrange("p t (j d) -> p t j d", j=2)[:, :, :, P]
        flat_weights = (LAYERS + 1) * GATES * P
        scratch_from = (NG - SCRATCH) * W
        wide = adjT[:, scratch_from:scratch_from + flat_weights].rearrange("p (l e) -> p l e", l=LAYERS + 1)
        msg_from = scratch_from + flat_weights
        msgT = adjT[:, msg_from:msg_from + LAYERS * P].rearrange("p (l k) -> p l k", l=LAYERS)
        ihT = adjT[:, msg_from + LAYERS * P:msg_from + (LAYERS + GATES) * P]
        fold = [ps2[0][:, 0], ps2[0][:, 1], ps2[1][:, 0], ps2[1][:, 1],
                ps1[:].rearrange("p (t j) d -> p t (j d)", t=2)[:, 0]]
        ext = sb("ext", [P, 2])
        ext_all = sb("ext_all", [P, 2])
        top = sb("top", [P, 4])
        wscale = sb("wscale", [P, 1])
        bih = sb("bih", [P, GATES])
        bhh = sb("bhh", [P, GATES])
        fold_loaded = sem("fold_loaded")
        gates_loaded, ident0, ident_ok, folded, copied, extremes, spread, link, split_done = (
            sem(n) for n in "gates_loaded ident0 ident_ok folded copied extremes spread link split_done".split())
        w_loaded = sem("l0_w_loaded")
        x_loaded = [sem(f"x_loaded{b}") for b in range(RING)]
        adj_loaded = [sem(f"adj_loaded{b}") for b in range(RING)]
        kept = [sem(f"kept{b}") for b in range(RING)]
        (stats_done, moments_done, var_ready, rstd_ready, centred, rows_ready, pattern_done, rows_turned,
         adj_turned, hT_done, aT_done, first_done, u_done, own_done, sums_done,
         ones_set, biased, row_done, rinv_done, second_done, gathered, x_done) = (
            sem("l0_" + n) for n in (
                "stats_done moments_done var_ready rstd_ready centred rows_ready pattern_done rows_turned "
                "adj_turned hT_done aT_done first_done u_done own_done "
                "sums_done ones_set biased row_done rinv_done second_done gathered x_done").split())
        block = ctx.enter_context(nc.Block())

        @block.sync
        def _(sp):
            def load_weights():
                for dst, src in ((wide[:, LAYERS, :], c["hhT_in"]), (bih[:], c["bih_in"]),
                                 (bhh[:], c["bhh_in"]), (c["mask"][:], c["mask_in"])):
                    sp.dma_start(dst, src).then_inc(gates_loaded, 16)
                sp.dma_start(wcat[:], c["l0_w_in"].rearrange("(t k) o -> k t o", t=2)).then_inc(w_loaded, 16)
                sp.dma_start(bias[:, 0], c["l0_b_in"]).then_inc(w_loaded, 16)

            def scratch_free():
                sp.wait_ge(split_done, 1)

            def load(q, b):
                g = RING * q + b
                after(sp, stats_done, g - 3)
                nc.sync.nop(nofuse=True)
                sp.dma_start(graphs(cols(x, g)), c["x_in"][bass.ts(g, GB)].rearrange("b n d -> n b d"))\
                  .then_inc(x_loaded[b], 16)
                after(sp, adj_turned, g - 3)
                after(sp, pattern_done, g - 3)
                nc.sync.nop(nofuse=True)
                sp.dma_start(adj[b][:], c["adj_in"][bass.ts(g, GB)].rearrange("b n d -> n b d"))\
                  .then_inc(adj_loaded[b], 16)

            def keep(q, b):
                g = RING * q + b
                sp.wait_ge(aT_done, g + 1)
                nc.sync.nop(nofuse=True)
                sp.dma_start(graphs(cols(adjT, g)), aT[b % 2][:]).then_inc(kept[b], 16)

            staggered(sp, [(5, keep), (0, load), at_ticks({1: load_weights, RING + 7: scratch_free})])
            for b in range(RING):
                sp.wait_ge(kept[b], 16 * NG // RING)

        @block.gpsimd
        def _(pool):
            def centre(q, b):
                g = RING * q + b
                pool.wait_ge(var_ready, g + 1)
                after(pool, rows_turned, g - 3)
                nc.gpsimd.tensor_tensor(rstd[b][:], var[b % 2][:], c["minus_half"][:], ALU.pow)\
                  .then_inc(rstd_ready, 1)
                nc.gpsimd.tensor_tensor(hn[b][:], graphs(cols(x, g)), per_node(mv[b % 2][:, :, 0:1]),
                                        ALU.subtract).then_inc(centred, 1)

            def add_bias(q, b):
                g = RING * q + b
                pool.wait_ge(own_done, g + 1)
                nc.gpsimd.tensor_tensor(pre[b % 2][:], pre[b % 2][:], bias[:].to_broadcast([P, GB, P]),
                                        ALU.add).then_inc(biased, 1)

            def reduce_extremes():
                pool.wait_ge(extremes, 2)
                nc.gpsimd.partition_all_reduce(ext_all[:], ext[:], P,
                                               bass.bass_isa.ReduceOp.absmax).then_inc(spread, 1)

            nc.gpsimd.memset(c["ident"][:], 0.0).then_inc(ident0, 1)
            pool.wait_ge(ident0, 1)
            nc.gpsimd.affine_select(out=c["ident"][:], in_=c["ident"][:], compare_op=ALU.not_equal, fill=1.0,
                                    base=0, pattern=[[-1, P]], channel_multiplier=1).then_inc(ident_ok, 1)
            pool.wait_ge(ones_set, 3)
            staggered(pool, [(6, add_bias), (1, centre), at_ticks({8: reduce_extremes})])

        @block.vector
        def _(dve):
            def of(q, b):
                g = RING * q + b
                return statistics(nc, dve, lambda j: cols(x, g, j), stats[b % 2], stats_done, mv[b % 2],
                                  moments_done, var[b % 2][:], var_ready, g + 1)

            def raw(q, b):
                g = RING * q + b
                dve.wait_ge(x_loaded[b], dma_count(q, b, 0)[1])
                after(dve, centred, g - 1)
                of(q, b)[0]()

            def binary(q, b):
                g = RING * q + b
                dve.wait_ge(adj_loaded[b], dma_count(q, b, 0)[1])
                nc.vector.tensor_scalar(graphs(cols(pattern, g)), adj[b][:], 0.0, None, ALU.not_equal)\
                  .then_inc(pattern_done, 1)

            def row_sums(q, b):
                g = RING * q + b
                dve.wait_ge(second_done, g + 1)
                nc.vector.tensor_copy(sums[:, bass.ds(g * 2 * GB, GB)].rearrange("p (t j) -> p t j", t=2),
                                      row_part(b)).then_inc(sums_done, 1)

            def safe_sums(q, b):
                g = RING * q + b
                dve.wait_ge(sums_done, g + 1)
                nc.vector.tensor_scalar(rinv[b % 2][:], sums[:, bass.ds(g * 2 * GB, GB)], ROW_EPS, None, ALU.add)\
                  .then_inc(row_done, 1)

            def inverse(q, b):
                dve.wait_ge(row_done, RING * q + b + 1)
                nc.vector.reciprocal(rinv[b % 2][:], rinv[b % 2][:]).then_inc(rinv_done, 1)

            def gather(q, b):
                g = RING * q + b
                dve.wait_ge(biased, g + 1)
                dve.wait_ge(rinv_done, g + 1)
                for j in range(GB):
                    last = nc.vector.scalar_tensor_tensor(pre[b % 2][:, j, :], of_graph(b, j)[:, 0:P],
                                                          rinv[b % 2][:, j:j + 1], pre[b % 2][:, j, :],
                                                          ALU.mult, ALU.add)
                last.then_inc(gathered, 1)

            def close(q, b):
                g = RING * q + b
                dve.wait_ge(gathered, g + 1)
                nc.vector.scalar_tensor_tensor(cols(x, g), pre[b % 2][:].rearrange("p b d -> p (b d)"), 0.0,
                                               cols(x, g), ALU.max, ALU.add).then_inc(x_done, 1)

            flat = wide.rearrange("p l e -> p (l e)")
            w_hi, w_lo = (c[n][:].rearrange("p l e -> p (l e)") for n in ("w_hi", "w_lo"))
            count = [0]

            def linked(ins):
                count[0] += 1
                ins.then_inc(link, 1)
                dve.wait_ge(link, count[0])

            def copy_folded():
                for l in range(LAYERS):
                    dve.wait_ge(folded, l + 1)
                    nc.vector.tensor_copy(wide[:, l, :], fold[l][:, 0:GATES * P]).then_inc(copied, 1)

            def extreme(side, op):
                def task():
                    dve.wait_ge(copied, LAYERS)
                    dve.wait_ge(gates_loaded, 4 * 16)
                    nc.vector.tensor_reduce(ext[:, side:side + 1], flat, AX, op).then_inc(extremes, 1)
                return task

            def scales():
                dve.wait_ge(spread, 1)
                linked(nc.vector.tensor_tensor(top[:, 1:2], ext_all[:, 0:1], ext_all[:, 1:2], ALU.max))
                linked(nc.vector.tensor_scalar(top[:, 2:3].bitcast(I32), top[:, 1:2].bitcast(I32), 0x7F800000,
                                               None, ALU.bitwise_and))
                linked(nc.vector.tensor_scalar(top[:, 0:1], top[:, 2:3], 2.0 ** -60, None, ALU.max))
                linked(nc.vector.reciprocal(top[:, 3:4], top[:, 0:1]))
                linked(nc.vector.tensor_scalar(wscale[:], top[:, 3:4], SW, None, ALU.mult))
                nc.vector.tensor_scalar(c["gscale"][:], top[:, 0:1], 1.0 / (SW * SH), None, ALU.mult)
                nc.vector.tensor_scalar(c["bhn"][:], bhh[:, 2:3], wscale[:], SH, ALU.mult, ALU.mult)
                nc.vector.tensor_tensor(c["brz"][:], bih[:, 0:2], bhh[:, 0:2], ALU.add)
                nc.vector.tensor_copy(c["bin"][:], bih[:, 2:3])

            def split_high():
                linked(nc.vector.tensor_scalar(w_hi, flat, wscale[:], None, ALU.mult))

            def split_low():
                nc.vector.scalar_tensor_tensor(w_lo, flat, wscale[:], w_hi, ALU.mult, ALU.subtract)\
                  .then_inc(split_done, 1)

            nc.vector.memset(c["minus_half"][:], -0.5).then_inc(ones_set, 1)
            for b in range(2):
                nc.vector.memset(u[b][:, :, P:P + 1], 1.0).then_inc(ones_set, 1)
            weight_tasks = {2: copy_folded, 5: extreme(0, ALU.max), 7: extreme(1, ALU.min), 9: scales,
                            10: split_high, 11: split_low}
            staggered(dve, [(1, raw), (6, row_sums), (1, lambda q, b: of(q, b)[1]()), (6, safe_sums),
                            (1, lambda q, b: of(q, b)[2]()), (6, inverse), (3, binary),
                            (6, gather), (6, close), at_ticks(weight_tasks)])
            dve.wait_ge(x_done, NG)

        @block.scalar
        def _(act):
            def scale(q, b):
                g = RING * q + b
                act.wait_ge(centred, g + 1)
                act.wait_ge(rstd_ready, g + 1)
                for j in range(GB):
                    last = nc.scalar.activation(hn[b][:, j, :], hn[b][:, j, :], ACT.Copy,
                                                scale=rstd[b][:, j:j + 1])
                last.then_inc(rows_ready, 1)

            def turned(q, b):
                g = RING * q + b
                act.wait_ge(rows_turned, g + 1)
                after(act, first_done, g - 1)
                nc.scalar.activation(hT[b % 2][:], psH[:], ACT.Relu).then_inc(hT_done, 1)
                act.wait_ge(adj_turned, g + 1)
                after(act, second_done, g - 1)
                before, count = dma_count(q, b, 2)
                after(act, kept[before], count)
                for j in range(GB):
                    last = nc.scalar.activation(aT[b % 2][:, j, :], psA[:, j, :], ACT.Copy,
                                                accum_out=sums[:, bass.ds(g * 2 * GB + GB + j, 1)])
                last.then_inc(aT_done, 1)

            def products(q, b):
                g = RING * q + b
                act.wait_ge(first_done, g + 1)
                after(act, second_done, g - 1)
                nc.scalar.activation(u[b % 2][:, :, 0:P], ps1[:, :, P:2 * P], ACT.Copy).then_inc(u_done, 1)
                after(act, x_done, g - 1)
                nc.scalar.activation(pre[b % 2][:], ps1[:, :, 0:P], ACT.Copy).then_inc(own_done, 1)

            for dst, src in ((msgT, c["msgT_in"].rearrange("l k c -> k l c")), (ihT, c["ihT_in"])):
                act.dma_start(dst, src).then_inc(fold_loaded, 16)
            staggered(act, [(4, turned), (5, products), (2, scale)])
            act.wait_ge(own_done, NG)

        @block.tensor
        def _(pe):
            def turn(q, b):
                g = RING * q + b
                pe.wait_ge(adj_loaded[b], dma_count(q, b, 0)[1])
                after(pe, aT_done, g)
                for j in range(GB):
                    last = nc.tensor.transpose(psA[:, j, :], adj[b][:, j, :], c["ident"][:])
                last.then_inc(adj_turned, 1)
                pe.wait_ge(rows_ready, g + 1)
                after(pe, hT_done, g)
                for j in range(GB):
                    last = nc.tensor.transpose(psH[:, j, :], hn[b][:, j, :], c["ident"][:])
                last.then_inc(rows_turned, 1)

            def first(q, b):
                g = RING * q + b
                pe.wait_ge(hT_done, g + 1)
                after(pe, own_done, g)
                for j in range(GB):
                    last = nc.tensor.matmul(ps1[:, j, :], hT[b % 2][:, j, :],
                                            wcat[:].rearrange("k t o -> k (t o)"), start=True, stop=True)
                last.then_inc(first_done, 1)

            def second(q, b):
                g = RING * q + b
                pe.wait_ge(u_done, g + 1)
                after(pe, gathered, g - 1)
                for j in range(GB):
                    last = nc.tensor.matmul(of_graph(b, j), aT[b % 2][:, j, :], u[b % 2][:, j, :],
                                            start=True, stop=True)
                last.then_inc(second_done, 1)

            pe.wait_ge(fold_loaded, 2 * 16)
            for l in range(LAYERS):
                nc.tensor.matmul(fold[l][:, 0:GATES * P], msgT[:, l, :], ihT, start=True, stop=True)\
                  .then_inc(folded, 1)
            pe.wait_ge(w_loaded, 32)
            pe.wait_ge(ident_ok, 1)
            pe.wait_ge(ones_set, 3)
            pe.wait_ge(copied, LAYERS)
            staggered(pe, [(4, turn), (6, second), (5, first)])


def layer1(nc, c):
    x, pattern, w_hi, w_lo, sums, no_sum = (c[n] for n in "x pattern w_hi w_lo sums no_sum".split())
    R_, Z_, N_ = range(GATES)
    with ExitStack() as ctx:
        sb = lambda name, shape, dt=F32: ctx.enter_context(nc.sbuf_tensor(name, shape, dt))
        sem = lambda name: ctx.enter_context(nc.semaphore(name))
        ps = lambda name: ctx.enter_context(nc.psum_tensor(name, [P, W], F32))
        state = [sb(f"state{j}", [P, W]) for j in range(SLOTS)]
        state_hi = [sb(f"state_hi{j}", [P, W], F16) for j in range(SLOTS)]
        state_lo = [sb(f"state_lo{j}", [P, W], F16) for j in range(SLOTS)]
        node_hi = [sb(f"node_hi{b}", [P, W], F16) for b in range(2)]
        node_lo = [sb(f"node_lo{b}", [P, W], F16) for b in range(2)]
        agg_hi = [sb(f"agg_hi{b}", [P, W], F16) for b in range(2)]
        agg_lo = [sb(f"agg_lo{b}", [P, W], F16) for b in range(2)]
        cand = [sb(f"cand{b}", [P, W]) for b in range(2)]
        zgate = [sb(f"zgate{b}", [P, W]) for b in range(2)]
        diff = sb("diff", [P, W])
        rows = sb("rows", [P, W])
        stats = sb("l1_stats", [P, GB, 6])
        left_words = pattern[:].bitcast(F32)
        left_stats = lambda group, j: left_words[:, bass.ds(group * (W // 2) + 6 * j, 6)]
        mv = sb("l1_mv", [P, SLOTS, GB, 2])
        var = sb("l1_var", [P, SLOTS, GB])
        rstd = sb("l1_rstd", [P, SLOTS, GB])
        psT = [ps(f"psT{b}") for b in range(2)]
        psQ = [ps(f"psQ{b}") for b in range(2)]
        psR, psZ, psI, psH = ps("psR"), ps("psZ"), ps("psI"), ps("psHn")
        (r_ready, z_ready, i_ready, h_ready, r_done, z_done, reset_done, pre_done, n_done, diff_done,
         gated, state_new) = (sem(n) for n in (
             "r_ready z_ready i_ready h_ready r_done z_done reset_done pre_done n_done diff_done "
             "gated state_new").split())
        (turned, node_hi_done, node_ready, agg_ready, agg_hi_done, agg_split, state_hi_done,
         state_ready) = (sem(n) for n in (
             "turned node_hi_done node_ready agg_ready agg_hi_done agg_split state_hi_done state_ready").split())
        (stats_done, moments_done, var_ready, rstd_ready, centred, rows_ready, out_turned, out_done) = (
            sem("l1_" + n) for n in (
                "stats_done moments_done var_ready rstd_ready centred rows_ready out_turned out_done").split())
        left_stats_done, x_stats_kept = sem("left_stats_done"), sem("x_stats_kept")
        no_sum_done, sums_safe, roots_done = sem("no_sum_done"), sem("sums_safe"), sem("roots_done")
        block = ctx.enter_context(nc.Block())


        def place(q, k):
            nth = k * STAGGER % SLOTS
            since = k - STAGGER * nth
            group = SLOTS * (q + since // QUAD) + nth
            busy = not isinstance(group, int) or 0 <= group < NG
            return busy, since % QUAD < SLOTS, group, since % QUAD // SLOTS

        def steps_before(q, k):
            if isinstance(q, int):
                return sum(place(0, p)[0] for p in range(QUAD * q + k))
            return q * QUAD + (k - EMPTY)

        def quads(eng, step):
            for k in range(QUAD):
                step(0, k)
            with eng.Fori(1, NQ - 1) as q:
                for k in range(QUAD):
                    step(q, k)
            for k in range(QUAD + STAGGER * (SLOTS - 1) - 1):
                step(NQ - 1, k)

        def enters(q, k, by):
            busy, new, group, _ = place(q, k + by)
            return busy and new, group

        def last_start(q, k):
            past = next(p for p in range(1, QUAD) if place(q, k - p)[1])
            return past, place(q, k - past)[2]

        def statistics_at(q, k, later):
            nth, odd = divmod(k - later - STATS_FROM, 2)
            if odd or not 0 <= nth < SLOTS or (isinstance(q, int) and q >= NQ - 1):
                return None
            return SLOTS * (q + 1) + nth, nth

        @block.tensor
        def _(pe):
            def gate(bank, gate_at, layer, hi, lo, start, stop):
                w_at = bass.ts(gate_at, P)
                nc.tensor.matmul(bank[:], w_hi[:, layer, w_at], hi, start=start, stop=False)
                nc.tensor.matmul(bank[:], w_hi[:, layer, w_at], lo, start=False, stop=False)
                return nc.tensor.matmul(bank[:], w_lo[:, layer, w_at], hi, start=False, stop=stop)

            def turn(bank, src):
                for j in range(GB):
                    last = nc.tensor.transpose(bank[:, bass.ts(j, P)], src[:, bass.ts(j, P)], c["ident"][:])
                return last

            def transposes(q, k):
                busy, new, group, _ = place(q, k)
                b = k % 2
                if new:
                    left = group - SLOTS
                    if not (isinstance(left, int) and left < 0):
                        pe.wait_ge(state_new, steps_before(q, k - SLOTS + 1))
                        pe.wait_ge(node_ready, steps_before(q, k - 1))
                        after(pe, out_done, left - 1)
                        turn(psT[b], state[k % SLOTS]).then_inc(out_turned, 1)
                    if busy:
                        pe.wait_ge(rows_ready, group + 1)
                        after(pe, node_ready, steps_before(q, k))
                        turn(psT[1 - b], rows).then_inc(turned, 1)
                elif busy:
                    pe.wait_ge(state_new, steps_before(q, k - SLOTS + 1))
                    after(pe, node_ready, steps_before(q, k - 1))
                    past, started = last_start(q, k)
                    if past == 1 or isinstance(q, int):
                        pe.wait_ge(state_hi_done, steps_before(q, k - past + 1))
                    if past == 2 or isinstance(q, int):
                        after(pe, out_done, started - SLOTS + 1)
                    turn(psT[b], state[k % SLOTS]).then_inc(turned, 1)

            def aggregate(q, k):
                busy, _, group, _ = place(q, k)
                if not busy:
                    return
                b = k % 2
                pe.wait_ge(node_ready, steps_before(q, k + 1))
                after(pe, agg_split, steps_before(q, k - 1))
                for j in range(GB):
                    at = bass.ts(j, P)
                    nc.tensor.matmul(psQ[b][:, at], node_hi[b][:, at], cols(pattern, group, j),
                                     start=True, stop=False)
                    last = nc.tensor.matmul(psQ[b][:, at], node_lo[b][:, at], cols(pattern, group, j),
                                            start=False, stop=True)
                last.then_inc(agg_ready, 1)

            def step(q, k):
                busy, _, _, layer = place(q, k)
                slot, b = k % SLOTS, k % 2
                before, this = steps_before(q, k), steps_before(q, k + 1)
                hi, lo = state_hi[slot][:], state_lo[slot][:]
                if busy:
                    pe.wait_ge(state_ready, this)
                    after(pe, r_done, before)
                    gate(psR, R_, LAYERS, hi, lo, True, False)
                    after(pe, reset_done, before)
                    gate(psH, N_, LAYERS, hi, lo, True, True).then_inc(h_ready, 1)
                    after(pe, z_done, before)
                    gate(psZ, Z_, LAYERS, hi, lo, True, False)
                transposes(q, k + 2)
                if busy:
                    pe.wait_ge(agg_split, this)
                    gate(psR, R_, layer, agg_hi[b][:], agg_lo[b][:], False, True).then_inc(r_ready, 1)
                    after(pe, pre_done, before)
                    gate(psI, N_, layer, agg_hi[b][:], agg_lo[b][:], True, True).then_inc(i_ready, 1)
                aggregate(q, k + 1)
                if busy:
                    gate(psZ, Z_, layer, agg_hi[b][:], agg_lo[b][:], False, True).then_inc(z_ready, 1)

            transposes(0, 0)
            aggregate(0, 0)
            quads(pe, step)

        @block.scalar
        def _(act):
            def node_high(q, k):
                busy, new, group, _ = place(q, k)
                if not busy:
                    return
                b = k % 2
                if new:
                    act.wait_ge(rows_ready, group + 1)
                else:
                    act.wait_ge(turned, steps_before(q, k + 1))
                after(act, agg_ready, steps_before(q, k - 1))
                nc.scalar.activation(node_hi[b][:], rows[:] if new else psT[b][:], ACT.Copy, scale=SH)\
                  .then_inc(node_hi_done, 1)

            def first_state(q, k):
                if enters(q, k, 0)[0]:
                    slot, b = k % SLOTS, k % 2
                    act.wait_ge(turned, steps_before(q, k + 1))
                    nc.scalar.activation(state[slot][:], psT[1 - b][:], ACT.Copy)
                    nc.scalar.activation(state_hi[slot][:], psT[1 - b][:], ACT.Copy, scale=SH)\
                      .then_inc(state_hi_done, 1)

            def aggregate_hi(q, k):
                if place(q, k)[0]:
                    b = k % 2
                    act.wait_ge(agg_ready, steps_before(q, k + 1))
                    after(act, z_ready, steps_before(q, k - 1))
                    nc.scalar.activation(agg_hi[b][:], psQ[b][:], ACT.Copy).then_inc(agg_hi_done, 1)

            def step(q, k):
                busy = place(q, k)[0]
                b = k % 2
                before, this = steps_before(q, k), steps_before(q, k + 1)
                node_high(q, k + 2)
                if busy:
                    act.wait_ge(r_ready, this)
                    after(act, state_new, steps_before(q, k - 1))
                    nc.scalar.activation(cand[b][:], psR[:], ACT.Sigmoid, bias=c["brz"][:, 0:1],
                                         scale=c["gscale"][:]).then_inc(r_done, 1)
                aggregate_hi(q, k + 1)
                if busy:
                    act.wait_ge(z_ready, this)
                    after(act, gated, steps_before(q, k - 1))
                    nc.scalar.activation(zgate[b][:], psZ[:], ACT.Sigmoid, bias=c["brz"][:, 1:2],
                                         scale=c["gscale"][:]).then_inc(z_done, 1)
                first_state(q, k + 2)
                busy3, new3, _, _ = place(q, k + 3)
                if busy3 and not new3:
                    act.wait_ge(state_new, before)
                    slot = (k - 1) % SLOTS
                    nc.scalar.activation(state_hi[slot][:], state[slot][:], ACT.Copy, scale=SH)\
                      .then_inc(state_hi_done, 1)
                if busy:
                    act.wait_ge(pre_done, this)
                    nc.scalar.activation(cand[b][:], cand[b][:], ACT.Tanh, bias=c["bin"][:],
                                         scale=c["gscale"][:]).then_inc(n_done, 1)

            nc.scalar.preload_act_table_set("sigmoid_and_others")
            node_high(0, 0)
            first_state(0, 0)
            aggregate_hi(0, 0)
            quads(act, step)

        @block.gpsimd
        def _(pool):
            def root(group, nth):
                pool.wait_ge(var_ready, group + 1)
                after(pool, rows_ready, group - SLOTS + 1)
                nc.gpsimd.tensor_tensor(rstd[:, nth, :], var[:, nth, :], c["minus_half"][:], ALU.pow)\
                  .then_inc(rstd_ready, 1)

            def centre(q, k, group):
                nth = k * STAGGER % SLOTS
                if not (isinstance(group, int) and group == 0):
                    entered = steps_before(q, k - last_start(q, k)[0] + 1)
                    pool.wait_ge(turned, entered)
                    pool.wait_ge(node_ready, entered)
                pool.wait_ge(moments_done, group + 1)
                nc.gpsimd.tensor_tensor(graphs(rows[:]), graphs(cols(x, group)), per_node(mv[:, nth, :, 0:1]),
                                        ALU.subtract).then_inc(centred, 1)

            def root_of_sums(q, part):
                at = sums[:, bass.ds(q * 2 * GB * SLOTS + part * GB, GB)]
                nc.gpsimd.tensor_tensor(at, at, c["minus_half"][:], ALU.pow).then_inc(roots_done, 1)

            def step(q, k):
                busy = place(q, k)[0]
                slot, b = k % SLOTS, k % 2
                before, this = steps_before(q, k), steps_before(q, k + 1)
                if busy:
                    pool.wait_ge(n_done, this)
                    after(pool, state_new, before)
                    nc.gpsimd.tensor_tensor(diff[:], state[slot][:], cand[b][:], ALU.subtract)\
                      .then_inc(diff_done, 1)
                    pool.wait_ge(diff_done, this)
                    pool.wait_ge(z_done, this)
                    nc.gpsimd.tensor_tensor(diff[:], diff[:], zgate[b][:], ALU.mult).then_inc(gated, 1)
                if statistics_at(q, k, 2):
                    root(*statistics_at(q, k, 2))
                if enters(q, k, CENTRE_AHEAD)[0]:
                    centre(q, k + CENTRE_AHEAD, enters(q, k, CENTRE_AHEAD)[1])
                if k in sum_places:
                    root_of_sums(q, sum_places.index(k))

            sum_places = (2, 3, 6, 7, 8, 9, 11, 13)
            root(0, 0)
            centre(0, 0, 0)
            for nth in range(1, SLOTS):
                root(nth, nth)
            centre(0, STAGGER, 1)
            pool.wait_ge(sums_safe, 1)
            quads(pool, step)
            pool.wait_ge(roots_done, NQ * 2 * SLOTS)

        @block.vector
        def _(dve):
            def of(group, nth):
                return statistics(nc, dve, lambda j: cols(x, group, j), stats, stats_done, mv[:, nth],
                                  moments_done, var[:, nth, :], var_ready, group + 1)

            def raw(group, nth):
                after(dve, moments_done, group)
                of(group, nth)[0]()

            def moments(group, nth):
                after(dve, centred, group - SLOTS + 1)
                _, moments_, variance_ = of(group, nth)
                moments_()
                after(dve, rstd_ready, group - SLOTS + 1)
                variance_()

            def make_rows(group, nth):
                dve.wait_ge(centred, group + 1)
                dve.wait_ge(rstd_ready, group + 1)
                for j in range(GB):
                    last = nc.vector.tensor_scalar(rows[:, bass.ts(j, P)], rows[:, bass.ts(j, P)],
                                                   rstd[:, nth, j:j + 1], 0.0, ALU.mult, ALU.max)
                last.then_inc(rows_ready, 1)

            def node_low(q, k):
                busy, new, _, _ = place(q, k)
                if busy:
                    b = k % 2
                    dve.wait_ge(node_hi_done, steps_before(q, k + 1))
                    nc.vector.scalar_tensor_tensor(node_lo[b][:], rows[:] if new else psT[b][:], SH, node_hi[b][:],
                                                   ALU.mult, ALU.subtract).then_inc(node_ready, 1)

            def state_low(q, k):
                slot = k % SLOTS
                dve.wait_ge(state_hi_done, steps_before(q, k + 1))
                nc.vector.scalar_tensor_tensor(state_lo[slot][:], state[slot][:], SH, state_hi[slot][:],
                                               ALU.mult, ALU.subtract).then_inc(state_ready, 1)

            def aggregate_low(q, k):
                if place(q, k)[0]:
                    b = k % 2
                    dve.wait_ge(agg_hi_done, steps_before(q, k + 1))
                    nc.vector.tensor_tensor(agg_lo[b][:], psQ[b][:], agg_hi[b][:], ALU.subtract)\
                       .then_inc(agg_split, 1)

            def leave(group, b):
                dve.wait_ge(out_turned, group + 1)
                for j in range(GB):
                    last = nc.vector.scalar_tensor_tensor(
                        cols(x, group, j), psT[b][:, bass.ts(j, P)],
                        c["mask"][:, bass.ds(group * GB + j, 1)], cols(x, group, j), ALU.mult, ALU.add)
                last.then_inc(out_done, 1)

            def left_raw(group):
                dve.wait_ge(out_done, group + 1)
                for j in range(GB):
                    last = nc.vector.bn_stats(left_stats(group, j), cols(x, group, j))
                last.then_inc(left_stats_done, 1)

            def update(q, k):
                if place(q, k)[0]:
                    dve.wait_ge(gated, steps_before(q, k + 1))
                    nc.vector.tensor_tensor(state[k % SLOTS][:], cand[k % 2][:], diff[:], ALU.add)\
                      .then_inc(state_new, 1)

            def step(q, k):
                busy = place(q, k)[0]
                b = k % 2
                this = steps_before(q, k + 1)
                node_low(q, k + 2)
                if busy:
                    dve.wait_ge(r_done, this)
                    dve.wait_ge(h_ready, this)
                    nc.vector.scalar_tensor_tensor(cand[b][:], psH[:], c["bhn"][:], cand[b][:], ALU.add, ALU.mult)\
                      .then_inc(reset_done, 1)
                aggregate_low(q, k + 1)
                update(q, k - 1)
                if busy:
                    dve.wait_ge(reset_done, this)
                    dve.wait_ge(i_ready, this)
                    nc.vector.tensor_tensor(cand[b][:], cand[b][:], psI[:], ALU.add).then_inc(pre_done, 1)
                _, new2, group2, _ = place(q, k + 2)
                if enters(q, k, 2)[0]:
                    state_low(q, k + 2)
                busy3, new3, _, _ = place(q, k + 3)
                if busy3 and not new3:
                    state_low(q, k + 3)
                if new2 and not (isinstance(group2, int) and group2 < SLOTS):
                    leave(group2 - SLOTS, b)
                if statistics_at(q, k, 0):
                    raw(*statistics_at(q, k, 0))
                if statistics_at(q, k, 1):
                    moments(*statistics_at(q, k, 1))
                if not (isinstance(q, int) and q == 0):
                    at, back = (k, 1) if k < QUAD else (k - QUAD, 0)
                    if at in LEFT_STATS:
                        left_raw((q - back) * SLOTS + LEFT_STATS.index(at))
                starts, started = enters(q, k, ROWS_AHEAD)
                if starts:
                    make_rows(started, (k + ROWS_AHEAD) * STAGGER % SLOTS)

            nc.vector.tensor_scalar(no_sum[:], sums[:], 0.0, None, ALU.is_equal).then_inc(no_sum_done, 1)
            raw(0, 0)
            moments(0, 0)
            dve.wait_ge(no_sum_done, 1)
            nc.vector.tensor_tensor(sums[:], sums[:], no_sum[:], ALU.add).then_inc(sums_safe, 1)
            make_rows(0, 0)
            node_low(0, 0)
            state_low(0, 0)
            aggregate_low(0, 0)
            for nth in range(1, SLOTS):
                raw(nth, nth)
                moments(nth, nth)
            make_rows(1, 1)
            quads(dve, step)
            left_raw(NG - 1)
            dve.wait_ge(left_stats_done, NG)
            dve.wait_ge(z_ready, NG * LAYERS)
            nc.vector.tensor_copy(c["x_stats"].rearrange("p (g m) -> p g m", m=6 * GB),
                                  left_words.rearrange("p (g w) -> p g w", g=NG)[:, :, 0:6 * GB])\
              .then_inc(x_stats_kept, 1)
            dve.wait_ge(x_stats_kept, 1)


def layers_2_and_3(nc, c):
    HID = 2
    SHIFT = 2
    x, adjT, sums = c["x"], c["adjT"], c["sums"]
    with ExitStack() as ctx:
        sb = lambda name, shape, dt=F32: ctx.enter_context(nc.sbuf_tensor(name, shape, dt))
        sem = lambda name: ctx.enter_context(nc.semaphore(name))
        ring = lambda name, n, shape, dt=F32: [sb(f"l2_{name}{b}", shape, dt) for b in range(n)]
        ps = lambda name, shape: ctx.enter_context(nc.psum_tensor(name, shape, F32))
        wcat = sb("l2_wcat", [P, 2, P])
        gb = sb("l2_gb", [P, 2])
        has_sum = sb("l2_has_sum", [P, NG * 2 * GB])
        rows = ring("rows", RING, [P, GB, P])
        xn = ring("xn", RING, [P, GB, P])
        aS_u = sb("aS_u", [P, 2, 2, W])
        aS, u = ([aS_u[:, t, b].rearrange("p (b d) -> p b d", b=GB) for b in range(2)] for t in range(2))
        hid = [aS_u[:, b] for b in range(2)]
        xnT = ring("xnT", 2, [P, GB, P])
        own = ring("own", RING, [P, GB, P])
        pre = ring("pre", RING, [P, GB, P])
        soft = ring("soft", RING, [P, GB, P])
        stats = ring("stats", 2, [P, GB * 6])
        mv = ring("mv", 2, [P, GB, 2])
        inner = ring("inner", 2, [P, GB])
        stats2 = ring("stats2", 2, [P, GB, 6])
        mv2 = ring("mv2", RING, [P, GB, 2])
        var2 = ring("var2", 2, [P, GB])
        rstd2 = ring("rstd2", RING, [P, GB])
        psX = [ps(f"l2_psX{b}", [P, GB, P]) for b in range(2)]
        ps1 = [ps(f"l2_ps1{b}", [P, GB, 2 * P]) for b in range(2)]
        ps2 = [ps(f"l2_ps2{b}", [P, GB, P]) for b in range(2)]
        (w_loaded, w_link, w_ready, fetched, moments_done, inner_ready, rows_ready,
         stats2_done, moments2_done, var2_ready, rstd2_ready, centred, xn_ready, aS_ready, xn_turned, xnT_done,
         first_done, u_done, own_done, second_done, pre_done, abs_done, exp_done, log_done, soft_done,
         x_done) = (
            sem("l2_" + n) for n in (
                "w_loaded w_link w_ready fetched moments_done inner_ready rows_ready "
                "stats2_done moments2_done var2_ready rstd2_ready centred xn_ready aS_ready xn_turned xnT_done "
                "first_done u_done own_done second_done pre_done abs_done exp_done log_done soft_done "
                "x_done").split())
        ring = lambda name, n, shape, dt=F32: [sb(f"l3_{name}{b}", shape, dt) for b in range(n)]
        w1 = sb("l3_w1", [P, HID, P])
        w2 = sb("l3_w2", [P, HID, P])
        b1 = sb("l3_b1", [P, HID])
        b2 = sb("l3_b2", [P, GB, P])
        eps1 = sb("l3_eps1", [P, 1])
        self_loop = sb("l3_self_loop", [P, GB, P])
        rows3 = ring("rows", RING, [P, GB, P])
        stats3 = ring("stats", 2, [P, GB, 6])
        mv3 = ring("mv", RING, [P, GB, 2])
        var3 = ring("var", 2, [P, GB])
        rstd3 = ring("rstd", RING, [P, GB])
        stored = [sem(f"l3_stored{b}") for b in range(RING)]
        (w3_loaded, eps_ready, loop_ready, stats3_done, moments3_done, var3_ready, rstd3_ready, normed, rows3_ready,
         aI_ready, mixed, gT_done, hidden, hid_done, projected, summed, out_ready) = (
            sem("l3_" + n) for n in (
                "w_loaded eps_ready loop_ready stats3_done moments3_done var3_ready rstd3_ready normed rows3_ready "
                "aI_ready mixed gT_done hidden hid_done projected summed out_ready").split())
        flat = lambda tile: tile[:].rearrange("p b d -> p (b d)")
        aI, gT, out = rows, [flat(tile) for tile in xnT], own
        psG, psO = [flat(tile) for tile in psX], ps2
        psA = [tile[:].rearrange("p (t j) d -> p t (j d)", t=HID) for tile in ps1]
        block = ctx.enter_context(nc.Block())

        @block.sync
        def _(sp):
            sp.dma_start(wcat[:, 0, :], c["l2_ws_in"]).then_inc(w_loaded, 16)
            sp.dma_start(wcat[:, 1, :], c["l2_wn_in"]).then_inc(w_loaded, 16)
            sp.dma_start(gb[:], c["l2_gb_in"]).then_inc(w_loaded, 16)
            for dst, src in ((w1[:], c["l3_w1_in"].rearrange("k (t o) -> k t o", t=HID)),
                             (w2[:], c["l3_w2_in"].rearrange("(t k) o -> k t o", t=HID)),
                             (b1[:], c["l3_b1_in"]), (b2[:], c["l3_b2_in"].rearrange("p (b d) -> p b d", b=GB)),
                             (eps1[:], c["l3_eps_in"])):
                sp.dma_start(dst, src).then_inc(w3_loaded, 16)

            def store(q, b):
                g = RING * q + b
                sp.wait_ge(out_ready, g + 1)
                sp.dma_start(c["out"][bass.ts(g, GB)].rearrange("b n d -> n b d"), out[b][:])\
                  .then_inc(stored[b], 16)

            staggered(sp, [(0, store)])
            for b in range(RING):
                sp.wait_ge(stored[b], 16 * NG // RING)

        @block.gpsimd
        def _(pool):
            def root2(q, b):
                g = RING * q + b
                pool.wait_ge(var2_ready, g + 1)
                nc.gpsimd.tensor_tensor(rstd2[b][:], var2[b % 2][:], c["minus_half"][:], ALU.pow)\
                  .then_inc(rstd2_ready, 1)

            def centre(q, b):
                g = RING * q + b
                pool.wait_ge(moments2_done, g + 1)
                after(pool, xn_turned, g - 3)
                nc.gpsimd.tensor_tensor(xn[b][:], rows[b][:], per_node(mv2[b][:, :, 0:1]), ALU.subtract)\
                  .then_inc(centred, 1)

            def scale_adj(q, b):
                g = RING * q + b
                if isinstance(q, int) and q == 0:
                    pool.wait_ge(w_ready, 1)
                after(pool, second_done, g - 1)
                s_in = sums[:, bass.ds(g * 2 * GB, GB)].rearrange("p (j o) -> p j o", o=1)
                nc.gpsimd.tensor_tensor(aS[b % 2][:], graphs(cols(adjT, g)), per_node(s_in), ALU.mult)\
                  .then_inc(aS_ready, 1)

            def add(q, b):
                g = RING * q + b
                pool.wait_ge(soft_done, g + 1)
                nc.gpsimd.tensor_tensor(graphs(cols(x, g)), graphs(cols(x, g)), soft[b][:], ALU.add)\
                  .then_inc(x_done, 1)

            def root3(q, b):
                g = RING * q + b
                pool.wait_ge(var3_ready, g + 1)
                nc.gpsimd.tensor_tensor(rstd3[b][:], var3[b % 2][:], c["minus_half"][:], ALU.pow)\
                  .then_inc(rstd3_ready, 1)

            def loops(q, b):
                g = RING * q + b
                if isinstance(q, int) and q == 0:
                    pool.wait_ge(loop_ready, GB)
                    pool.wait_ge(centred, NG)
                    pool.wait_ge(stats2_done, NG)
                after(pool, mixed, g - 3)
                nc.gpsimd.tensor_tensor(aI[b][:], graphs(cols(adjT, g)), self_loop[:], ALU.add)\
                  .then_inc(aI_ready, 1)

            def add_b2(q, b):
                g = RING * q + b
                pool.wait_ge(summed, g + 1)
                nc.gpsimd.tensor_tensor(out[b][:], out[b][:], b2[:], ALU.add).then_inc(out_ready, 1)

            staggered(pool, [(10, add), (2, centre), (2, root2), (5, scale_adj)],
                      [(7, add_b2), (0, root3), (1, loops)], SHIFT)

        @block.vector
        def _(dve):
            def fetch(q, b):
                g = RING * q + b
                after(dve, moments_done, g - 1)
                nc.vector.tensor_copy(stats[b % 2][:], c["x_stats"][:, bass.ds(g * 6 * GB, 6 * GB)])\
                  .then_inc(fetched, 1)

            def moments(q, b):
                g = RING * q + b
                after(dve, rows_ready, g - 1)
                after(dve, inner_ready, g - 1)
                dve.wait_ge(fetched, g + 1)
                nc.vector.nop(nofuse=True)
                for j in range(GB):
                    last = nc.vector.bn_aggr(mv[b % 2][:, j, :], stats[b % 2][:, bass.ts(j, 6)])
                last.then_inc(moments_done, 1)

            def clip(q, b):
                g = RING * q + b
                dve.wait_ge(moments_done, g + 1)
                after(dve, centred, g - 3)
                for j in range(GB):
                    last = nc.vector.tensor_scalar(rows[b][:, j, :], cols(x, g, j), mv[b % 2][:, j, 0:1], 0.0,
                                                   ALU.subtract, ALU.max)
                last.then_inc(rows_ready, 1)
                after(dve, var2_ready, g - 1)
                nc.vector.tensor_scalar(inner[b % 2][:], mv[b % 2][:, :, 1], LN_EPS, LN_EPS ** 2,
                                        ALU.mult, ALU.add).then_inc(inner_ready, 1)

            def raw2(q, b):
                g = RING * q + b
                dve.wait_ge(rows_ready, g + 1)
                for j in range(GB):
                    last = nc.vector.bn_stats(stats2[b % 2][:, j, :], rows[b][:, j, :])
                last.then_inc(stats2_done, 1)

            def moments2(q, b):
                g = RING * q + b
                dve.wait_ge(stats2_done, g + 1)
                nc.vector.nop(nofuse=True)
                for j in range(GB):
                    last = nc.vector.bn_aggr(mv2[b][:, j, :], stats2[b % 2][:, j, :])
                last.then_inc(moments2_done, 1)

            def variance2(q, b):
                g = RING * q + b
                dve.wait_ge(moments2_done, g + 1)
                dve.wait_ge(inner_ready, g + 1)
                after(dve, rstd2_ready, g - 1)
                nc.vector.tensor_tensor(var2[b % 2][:], mv2[b][:, :, 1], inner[b % 2][:], ALU.add)\
                  .then_inc(var2_ready, 1)

            def outer(q, b):
                g = RING * q + b
                dve.wait_ge(second_done, g + 1)
                dve.wait_ge(own_done, g + 1)
                for j in range(GB):
                    last = nc.vector.scalar_tensor_tensor(pre[b][:, j, :], ps2[b % 2][:, j, :],
                                                          sums[:, bass.ds(g * 2 * GB + GB + j, 1)],
                                                          own[b][:, j, :], ALU.mult, ALU.add)
                last.then_inc(pre_done, 1)

            def finish(q, b):
                g = RING * q + b
                dve.wait_ge(log_done, g + 1)
                flat = lambda tile: tile[:].rearrange("p b d -> p (b d)")
                nc.vector.scalar_tensor_tensor(flat(soft[b]), flat(pre[b]), 0.0, flat(soft[b]),
                                               ALU.max, ALU.add).then_inc(soft_done, 1)

            def of_x3(q, b):
                g = RING * q + b
                return statistics(nc, dve, lambda j: cols(x, g, j), stats3[b % 2], stats3_done, mv3[b],
                                  moments3_done, var3[b % 2][:], var3_ready, g + 1)

            def raw3(q, b):
                dve.wait_ge(x_done, RING * q + b + 1)
                after(dve, rstd3_ready, RING * q + b - 1)
                of_x3(q, b)[0]()

            def norm3(q, b):
                g = RING * q + b
                dve.wait_ge(rstd3_ready, g + 1)
                after(dve, mixed, g - 3)
                for j in range(GB):
                    last = nc.vector.tensor_scalar(rows3[b][:, j, :], cols(x, g, j), mv3[b][:, j, 0:1],
                                                   rstd3[b][:, j:j + 1], ALU.subtract, ALU.mult)
                last.then_inc(normed, 1)

            def clip3(q, b):
                dve.wait_ge(normed, RING * q + b + 1)
                nc.vector.tensor_scalar(rows3[b][:], rows3[b][:], 0.0, None, ALU.max).then_inc(rows3_ready, 1)

            def finish3(q, b):
                g = RING * q + b
                dve.wait_ge(projected, g + 1)
                if isinstance(q, int) and q == 0:
                    dve.wait_ge(pre_done, NG)
                before, count = dma_count(q, b, RING)
                after(dve, stored[before], count)
                nc.vector.tensor_tensor(out[b][:], psO[b % 2][:], graphs(cols(x, g)), ALU.add)\
                  .then_inc(summed, 1)

            def self_loops():
                dve.wait_ge(w3_loaded, 5 * 16)
                nc.vector.tensor_scalar(eps1[:], eps1[:], 1.0, None, ALU.add).then_inc(eps_ready, 1)
                dve.wait_ge(eps_ready, 1)
                for j in range(GB):
                    nc.vector.tensor_scalar(self_loop[:, j, :], c["ident"][:], eps1[:], None, ALU.mult)\
                      .then_inc(loop_ready, 1)

            def factors():
                dve.wait_ge(w_loaded, 48)
                nc.vector.tensor_tensor(wcat[:, 0, :], wcat[:, 0, :], wcat[:, 1, :], ALU.add)
                nc.vector.tensor_scalar(has_sum[:], c["no_sum"][:], -1.0, 1.0, ALU.mult, ALU.add).then_inc(w_link, 1)
                dve.wait_ge(w_link, 1)
                nc.vector.tensor_tensor(sums[:], sums[:], has_sum[:], ALU.mult).then_inc(w_link, 1)
                dve.wait_ge(w_link, 2)
                outer_part = sums[:].rearrange("p (g t j) -> p g t j", t=2, j=GB)[:, :, 1, :]
                nc.vector.tensor_scalar(outer_part, outer_part, -1.0, None, ALU.mult).then_inc(w_ready, 1)
                dve.wait_ge(w_ready, 1)

            staggered(dve, [(9, finish), (1, clip), (0, fetch), (7, outer), (1, raw2), (0, moments),
                            (1, moments2), (1, variance2), at_ticks({2: factors, 3: self_loops})],
                      [(0, raw3), (1, norm3), (0, lambda q, b: of_x3(q, b)[1]()), (1, clip3), (6, finish3),
                       (0, lambda q, b: of_x3(q, b)[2]())], SHIFT)

        @block.scalar
        def _(act):
            def scale(q, b):
                g = RING * q + b
                act.wait_ge(centred, g + 1)
                act.wait_ge(rstd2_ready, g + 1)
                for j in range(GB):
                    last = nc.scalar.activation(xn[b][:, j, :], xn[b][:, j, :], ACT.Copy,
                                                scale=rstd2[b][:, j:j + 1])
                last.then_inc(xn_ready, 1)

            def turned(q, b):
                g = RING * q + b
                act.wait_ge(xn_turned, g + 1)
                after(act, first_done, g - 1)
                nc.scalar.activation(xnT[b % 2][:], psX[b % 2][:], ACT.Identity, bias=gb[:, 1:2],
                                     scale=gb[:, 0:1]).then_inc(xnT_done, 1)

            def products(q, b):
                g = RING * q + b
                act.wait_ge(first_done, g + 1)
                after(act, second_done, g - 1)
                nc.scalar.activation(u[b % 2][:], ps1[b % 2][:, :, P:2 * P], ACT.Copy).then_inc(u_done, 1)
                after(act, pre_done, g - 3)
                nc.scalar.activation(own[b][:], ps1[b % 2][:, :, 0:P], ACT.Copy).then_inc(own_done, 1)

            def magnitude(q, b):
                g = RING * q + b
                act.wait_ge(pre_done, g + 1)
                after(act, x_done, g - 3)
                nc.scalar.activation(soft[b][:], pre[b][:], ACT.Abs).then_inc(abs_done, 1)

            def exponential(q, b):
                act.wait_ge(abs_done, RING * q + b + 1)
                nc.scalar.activation(soft[b][:], soft[b][:], ACT.Exp, scale=-1.0).then_inc(exp_done, 1)

            def logarithm(q, b):
                act.wait_ge(exp_done, RING * q + b + 1)
                nc.scalar.activation(soft[b][:], soft[b][:], ACT.Ln, bias=1.0).then_inc(log_done, 1)

            def mixed_rows(q, b):
                g = RING * q + b
                act.wait_ge(mixed, g + 1)
                if isinstance(q, int) and q == 0:
                    act.wait_ge(first_done, NG)
                after(act, hidden, g - 1)
                nc.scalar.activation(gT[b % 2][:], psG[b % 2][:], ACT.Copy).then_inc(gT_done, 1)

            def hidden_rows(q, b):
                g = RING * q + b
                act.wait_ge(hidden, g + 1)
                if isinstance(q, int) and q == 0:
                    act.wait_ge(second_done, NG)
                after(act, projected, g - 1)
                for t in range(HID):
                    last = nc.scalar.activation(hid[b % 2][:, t, :], psA[b % 2][:, t, :], ACT.Relu,
                                                bias=b1[:, t:t + 1])
                last.then_inc(hid_done, 1)

            nc.scalar.preload_act_table_set("natural_log_exp_and_others")
            act.wait_ge(w_loaded, 48)
            act.wait_ge(w3_loaded, 5 * 16)
            staggered(act, [(4, turned), (8, magnitude), (3, scale), (8, exponential), (5, products),
                            (8, logarithm)],
                      [(3, hidden_rows), (2, mixed_rows)], SHIFT)

        @block.tensor
        def _(pe):
            def turn(q, b):
                g = RING * q + b
                pe.wait_ge(xn_ready, g + 1)
                after(pe, xnT_done, g - 1)
                for j in range(GB):
                    last = nc.tensor.transpose(psX[b % 2][:, j, :], xn[b][:, j, :], c["ident"][:])
                last.then_inc(xn_turned, 1)

            def first(q, b):
                g = RING * q + b
                pe.wait_ge(xnT_done, g + 1)
                after(pe, own_done, g - 1)
                for j in range(GB):
                    last = nc.tensor.matmul(ps1[b % 2][:, j, :], xnT[b % 2][:, j, :],
                                            wcat[:].rearrange("k t o -> k (t o)"), start=True, stop=True)
                last.then_inc(first_done, 1)

            def second(q, b):
                g = RING * q + b
                pe.wait_ge(u_done, g + 1)
                pe.wait_ge(aS_ready, g + 1)
                after(pe, pre_done, g - 1)
                for j in range(GB):
                    last = nc.tensor.matmul(ps2[b % 2][:, j, :], aS[b % 2][:, j, :], u[b % 2][:, j, :],
                                            start=True, stop=True)
                last.then_inc(second_done, 1)

            def mix(q, b):
                g = RING * q + b
                pe.wait_ge(rows3_ready, g + 1)
                pe.wait_ge(aI_ready, g + 1)
                if isinstance(q, int) and q == 0:
                    pe.wait_ge(xnT_done, NG)
                after(pe, gT_done, g - 1)
                for j in range(GB):
                    last = nc.tensor.matmul(psG[b % 2][:, bass.ts(j, P)], rows3[b][:, j, :], aI[b][:, j, :],
                                            start=True, stop=True)
                last.then_inc(mixed, 1)

            def hide(q, b):
                g = RING * q + b
                pe.wait_ge(gT_done, g + 1)
                if isinstance(q, int) and q == 0:
                    pe.wait_ge(own_done, NG)
                after(pe, hid_done, g - 1)
                for t in range(HID):
                    last = nc.tensor.matmul(psA[b % 2][:, t, :], w1[:, t, :], gT[b % 2][:], start=True, stop=True)
                last.then_inc(hidden, 1)

            def project(q, b):
                g = RING * q + b
                pe.wait_ge(hid_done, g + 1)
                if isinstance(q, int) and q == 0:
                    pe.wait_ge(pre_done, NG)
                after(pe, summed, g - 1)
                for j in range(GB):
                    for t in range(HID):
                        last = nc.tensor.matmul(psO[b % 2][:, j, :], hid[b % 2][:, t, bass.ts(j, P)], w2[:, t, :],
                                                start=(t == 0), stop=(t == HID - 1))
                last.then_inc(projected, 1)

            pe.wait_ge(w_ready, 1)
            pe.wait_ge(w3_loaded, 5 * 16)
            staggered(pe, [(4, turn), (6, second), (5, first)], [(5, project), (3, hide), (2, mix)], SHIFT)


def gnn_stack_kernel(nc, c):
    with ExitStack() as ctx:
        sb = lambda name, shape, dt=F32: ctx.enter_context(nc.sbuf_tensor(name, shape, dt))
        c["x"] = sb("x", [P, NG * W])
        c["adjT"] = sb("adjT", [P, NG * W])
        c["sums"] = sb("sums", [P, NG * 2 * GB])
        c["no_sum"] = sb("no_sum", [P, NG * 2 * GB], mybir.dt.uint8)
        c["w_hi"] = sb("w_hi", [P, LAYERS + 1, GATES * P], F16)
        c["x_stats"] = c["w_hi"][:].rearrange("p l e -> p (l e)")[:, 0:2 * NG * GB * 6].bitcast(F32)
        c["ident"] = sb("ident", [P, P])
        c["minus_half"] = sb("minus_half", [P, GB])
        c["mask"] = sb("mask", [P, GRAPHS])
        c["gscale"] = sb("gscale", [P, 1])
        c["bhn"] = sb("bhn", [P, 1])
        c["brz"] = sb("brz", [P, 2])
        c["bin"] = sb("bin", [P, 1])
        with ExitStack() as until_l2:
            early = lambda name, shape: until_l2.enter_context(nc.sbuf_tensor(name, shape, F16))
            c["pattern"] = early("pattern", [P, NG * W])
            c["w_lo"] = early("w_lo", [P, LAYERS + 1, GATES * P])
            layer0(nc, c)
            layer1(nc, c)
        layers_2_and_3(nc, c)


def kernel(**inputs):
    import numpy as np
    import concourse.bacc as bacc
    from concourse.bass_utils import run_bass_kernel_spmd

    a = {k: np.asarray(v) for k, v in inputs.items()}
    column = lambda v, n: np.ascontiguousarray(v.reshape(n, P).T)
    spread = lambda v: np.ascontiguousarray(np.broadcast_to(np.tile(v, GB), (P, W)))
    arrays = {
        "x_in": a["x"], "adj_in": a["adj"],
        "mask_in": np.ascontiguousarray(a["nodemask"].T),
        "l0_w_in": a["L0_gnn_weight"], "l0_b_in": np.ascontiguousarray(np.broadcast_to(a["L0_gnn_bias"], (P, P))),
        "msgT_in": np.ascontiguousarray(a["L1_gnn_weight"].transpose(0, 2, 1)),
        "ihT_in": np.ascontiguousarray(a["L1_gnn_w_ih"].T), "hhT_in": np.ascontiguousarray(a["L1_gnn_w_hh"].T),
        "bih_in": column(a["L1_gnn_b_ih"], GATES), "bhh_in": column(a["L1_gnn_b_hh"], GATES),
        "l2_ws_in": a["L2_gnn_W_self"], "l2_wn_in": a["L2_gnn_W_neigh"],
        "l2_gb_in": np.ascontiguousarray(np.stack([a["L2_gnn_gamma"], a["L2_gnn_beta"]], axis=1)),
        "l3_w1_in": a["L3_gnn_W1"], "l3_b1_in": column(a["L3_gnn_b1"], 2),
        "l3_w2_in": a["L3_gnn_W2"], "l3_b2_in": spread(a["L3_gnn_b2"]),
        "l3_eps_in": np.ascontiguousarray(np.broadcast_to(a["L3_gnn_eps"], (P, 1))),
    }
    nc = bacc.Bacc("TRN2", target_bir_lowering=False, num_devices=1)
    c = {n: nc.dram_tensor(n, v.shape, mybir.dt.from_np(v.dtype), kind="ExternalInput").ap()
         for n, v in arrays.items()}
    c["out"] = nc.dram_tensor("out", (GRAPHS, P, P), F32, kind="ExternalOutput").ap()
    gnn_stack_kernel(nc, c)
    r = run_bass_kernel_spmd(nc, [arrays], core_ids=[0])
    return r.results[0]["out"]
```
